# Optimizing a Trainium2 kernel written in Bass

```python
import numpy as np
import jax
import jax.numpy as jnp

def _softmax(x, axis=-1):
    return jax.nn.softmax(x, axis=axis)
def _gelu(x):
    return jax.nn.gelu(x, approximate=True)
def _silu(x):
    return jax.nn.silu(x)
def _sigmoid(x):
    return jax.nn.sigmoid(x)
def _layernorm(x, axis=-1, eps=1e-5):
    m = jnp.mean(x, axis=axis, keepdims=True)
    v = jnp.var(x, axis=axis, keepdims=True)
    return (x - m) / jnp.sqrt(v + eps)
def _scatter_add(tgt, idx, src, axis=0):
    return tgt.at[idx].add(src)
def _segment_sum(src, seg, n):
    return jax.ops.segment_sum(src, seg, n)

kernel_name = 'mk_adj_resnorm_d2_adj_128_1c81bb'

def setup_inputs(seed: int = 0):
    np.random.seed(seed)
    _w = jnp.asarray
    def _rec_inputs():
        import jax
        import jax.numpy as jnp
        _gk = jax.random.key(seed)
        x = -0.003407 + 1.001 * jax.random.normal(jax.random.fold_in(_gk, 1), (2708, 128), jnp.float32)
        _a = jax.random.bernoulli(jax.random.fold_in(_gk, 2), 0.0014771, (2708, 2708))
        _a = jnp.logical_or(_a, jnp.swapaxes(_a, -1, -2))
        _a = jnp.logical_or(_a, jnp.eye(2708, dtype=bool))
        _af = _a.astype(jnp.float32)
        _af = _af * jax.random.uniform(jax.random.fold_in(_gk, 3), (2708, 2708), jnp.float32, 0.05, 1)
        adj = _af
        return x, adj
    x, adj = _rec_inputs()
    def _L0_gnn_setup():
        import jax, jax.numpy as jnp
        import numpy as np
        LN_EPS = 1e-05
        key = jax.random.key(seed)
        ks = jax.random.split(key, 6)
        N, D = (1024, 128)
        return {'node_feats': jax.random.normal(ks[0], (N, D), dtype=jnp.float32), 'adj': jax.random.uniform(ks[1], (N, N), dtype=jnp.float32), 'msg_w': jax.random.normal(ks[2], (D, 2 * D), dtype=jnp.float32) * 0.05, 'msg_b': jax.random.normal(ks[3], (D,), dtype=jnp.float32) * 0.05, 'upd_w': jax.random.normal(ks[4], (D, 2 * D), dtype=jnp.float32) * 0.05, 'upd_b': jax.random.normal(ks[5], (D,), dtype=jnp.float32) * 0.05, 'ln_w': jnp.ones((D,), dtype=jnp.float32), 'ln_b': jnp.zeros((D,), dtype=jnp.float32)}
    _L0_gnn_all = _L0_gnn_setup()
    _L0_gnn_in = {k: v for k, v in _L0_gnn_all.items() if k in ('msg_w', 'msg_b', 'upd_w', 'upd_b', 'ln_w', 'ln_b', )}
    del _L0_gnn_all

    def _L1_gnn_setup():
        import jax, jax.numpy as jnp
        import numpy as np
        N, IN, H, C = (4096, 128, 4, 32)
        HC = H * C
        EDGE_P = 0.008

        def _linear_params(key, fan_in, fan_out, bias=True):
            k1, k2 = jax.random.split(key)
            lim = 1.0 / np.sqrt(fan_in)
            W = jax.random.uniform(k1, (fan_in, fan_out), jnp.float32, -lim, lim)
            if not bias:
                return W
            b = jax.random.uniform(k2, (fan_out,), jnp.float32, -lim, lim)
            return (W, b)

        def _transformer_conv(x, adj, Wq, bq, Wk, bk, Wv, bv, Ws, bs, Wb):
            n = x.shape[0]
            q = (x @ Wq + bq).reshape(n, H, C)
            k = (x @ Wk + bk).reshape(n, H, C)
            v = (x @ Wv + bv).reshape(n, H, C)
            attn = jnp.einsum('nhc,mhc->hnm', q, k) / np.float32(np.sqrt(C))
            mask = adj == 0.0
            neg = jnp.where(mask[None], -jnp.inf, attn)
            m = jnp.max(neg, axis=-1, keepdims=True)
            all_inf = jnp.isneginf(m)
            e = jnp.where(mask[None], 0.0, jnp.exp(neg - jnp.where(all_inf, 0.0, m)))
            denom = jnp.sum(e, axis=-1, keepdims=True)
            alpha = e / jnp.where(denom == 0.0, 1.0, denom)
            out = jnp.einsum('hnm,mhc->hnc', alpha, v)
            out = jnp.transpose(out, (1, 2, 0)).reshape(n, C * H)
            x_r = x @ Ws + bs
            beta = jax.nn.sigmoid(jnp.concatenate([out, x_r, out - x_r], axis=-1) @ Wb)
            return beta * x_r + (1.0 - beta) * out
        key = jax.random.key(seed)
        ks = jax.random.split(key, 7)
        x = jax.random.normal(ks[0], (N, IN), jnp.float32)
        adj = (jax.random.uniform(ks[1], (N, N)) < EDGE_P).astype(jnp.float32)
        Wq, bq = _linear_params(ks[2], IN, HC)
        Wk, bk = _linear_params(ks[3], IN, HC)
        Wv, bv = _linear_params(ks[4], IN, HC)
        Ws, bs = _linear_params(ks[5], IN, HC)
        Wb = _linear_params(ks[6], 3 * HC, 1, bias=False)
        return dict(x=x, adj=adj, Wq=Wq, bq=bq, Wk=Wk, bk=bk, Wv=Wv, bv=bv, Ws=Ws, bs=bs, Wb=Wb)
    _L1_gnn_all = _L1_gnn_setup()
    _L1_gnn_in = {k: v for k, v in _L1_gnn_all.items() if k in ('Wq', 'bq', 'Wk', 'bk', 'Wv', 'bv', 'Ws', 'bs', 'Wb', )}
    del _L1_gnn_all

    return {
        "x": x,
        "adj": adj,
        "L0_gnn_msg_w": _L0_gnn_in["msg_w"],
        "L0_gnn_msg_b": _L0_gnn_in["msg_b"],
        "L0_gnn_upd_w": _L0_gnn_in["upd_w"],
        "L0_gnn_upd_b": _L0_gnn_in["upd_b"],
        "L0_gnn_ln_w": _L0_gnn_in["ln_w"],
        "L0_gnn_ln_b": _L0_gnn_in["ln_b"],
        "L1_gnn_Wq": _L1_gnn_in["Wq"],
        "L1_gnn_bq": _L1_gnn_in["bq"],
        "L1_gnn_Wk": _L1_gnn_in["Wk"],
        "L1_gnn_bk": _L1_gnn_in["bk"],
        "L1_gnn_Wv": _L1_gnn_in["Wv"],
        "L1_gnn_bv": _L1_gnn_in["bv"],
        "L1_gnn_Ws": _L1_gnn_in["Ws"],
        "L1_gnn_bs": _L1_gnn_in["bs"],
        "L1_gnn_Wb": _L1_gnn_in["Wb"],
    }

def reference(x, adj, L0_gnn_msg_w, L0_gnn_msg_b, L0_gnn_upd_w, L0_gnn_upd_b, L0_gnn_ln_w, L0_gnn_ln_b, L1_gnn_Wq, L1_gnn_bq, L1_gnn_Wk, L1_gnn_bk, L1_gnn_Wv, L1_gnn_bv, L1_gnn_Ws, L1_gnn_bs, L1_gnn_Wb):
    import jax
    import jax.numpy as jnp
    def _L0_gnn_ref(node_feats, adj, msg_w, msg_b, upd_w, upd_b, ln_w, ln_b):
        import jax, jax.numpy as jnp
        import numpy as np
        LN_EPS = 1e-05
        D = node_feats.shape[-1]
        s = node_feats @ msg_w[:, :D].T
        d = node_feats @ msg_w[:, D:].T
        messages = jax.nn.gelu(s[:, None, :] + d[None, :, :] + msg_b, approximate=False)
        aggregated = jnp.einsum('ijd,ij->id', messages, adj)
        combined = jnp.concatenate([node_feats, aggregated], axis=-1)
        new_feats = combined @ upd_w.T + upd_b
        h = jax.nn.gelu(new_feats, approximate=False) + node_feats
        mu = jnp.mean(h, axis=-1, keepdims=True)
        var = jnp.var(h, axis=-1, keepdims=True)
        return (h - mu) / jnp.sqrt(var + LN_EPS) * ln_w + ln_b

    def _L1_gnn_ref(x, adj, Wq, bq, Wk, bk, Wv, bv, Ws, bs, Wb):
        import jax, jax.numpy as jnp
        import numpy as np
        N, IN, H, C = (4096, 128, 4, 32)
        HC = H * C
        EDGE_P = 0.008

        def _linear_params(key, fan_in, fan_out, bias=True):
            k1, k2 = jax.random.split(key)
            lim = 1.0 / np.sqrt(fan_in)
            W = jax.random.uniform(k1, (fan_in, fan_out), jnp.float32, -lim, lim)
            if not bias:
                return W
            b = jax.random.uniform(k2, (fan_out,), jnp.float32, -lim, lim)
            return (W, b)

        def _transformer_conv(x, adj, Wq, bq, Wk, bk, Wv, bv, Ws, bs, Wb):
            n = x.shape[0]
            q = (x @ Wq + bq).reshape(n, H, C)
            k = (x @ Wk + bk).reshape(n, H, C)
            v = (x @ Wv + bv).reshape(n, H, C)
            attn = jnp.einsum('nhc,mhc->hnm', q, k) / np.float32(np.sqrt(C))
            mask = adj == 0.0
            neg = jnp.where(mask[None], -jnp.inf, attn)
            m = jnp.max(neg, axis=-1, keepdims=True)
            all_inf = jnp.isneginf(m)
            e = jnp.where(mask[None], 0.0, jnp.exp(neg - jnp.where(all_inf, 0.0, m)))
            denom = jnp.sum(e, axis=-1, keepdims=True)
            alpha = e / jnp.where(denom == 0.0, 1.0, denom)
            out = jnp.einsum('hnm,mhc->hnc', alpha, v)
            out = jnp.transpose(out, (1, 2, 0)).reshape(n, C * H)
            x_r = x @ Ws + bs
            beta = jax.nn.sigmoid(jnp.concatenate([out, x_r, out - x_r], axis=-1) @ Wb)
            return beta * x_r + (1.0 - beta) * out
        return _transformer_conv(x, adj, Wq, bq, Wk, bk, Wv, bv, Ws, bs, Wb)

    x = _layernorm(x + _L0_gnn_ref(x, adj, L0_gnn_msg_w, L0_gnn_msg_b, L0_gnn_upd_w, L0_gnn_upd_b, L0_gnn_ln_w, L0_gnn_ln_b), axis=-1)
    x = _layernorm(x + _L1_gnn_ref(x, adj, L1_gnn_Wq, L1_gnn_bq, L1_gnn_Wk, L1_gnn_bk, L1_gnn_Wv, L1_gnn_bv, L1_gnn_Ws, L1_gnn_bs, L1_gnn_Wb), axis=-1)
    return x


_drawn_inputs = setup_inputs


def setup_inputs(seed=0):
    import zlib

    import numpy as np

    out = dict(_drawn_inputs(seed))
    spreads = {'L0_gnn_ln_w': (1.0, 0.2), 'L0_gnn_ln_b': (0.0, 0.1)}
    factors = {'L0_gnn_upd_b': 2.907, 'L1_gnn_bq': 8.0, 'L1_gnn_bk': 8.0}
    for name, (base, spread) in spreads.items():
        noise = np.random.default_rng([zlib.crc32(name.encode()), seed]).standard_normal(out[name].shape)
        drawn = base * np.exp(spread * noise) if base else spread * noise
        out[name] = jnp.asarray(drawn.astype(out[name].dtype))
    for name, factor in factors.items():
        out[name] = (out[name] * factor).astype(out[name].dtype)
    return out
```

```python
import concourse.bass as bass
from concourse import mybir
from contextlib import ExitStack

ALU = mybir.AluOpType
ACT = mybir.ActivationFunctionType
F32 = mybir.dt.float32
BF16 = mybir.dt.bfloat16
I32 = mybir.dt.int32
U32 = mybir.dt.uint32
AX = mybir.AxisListType

N = 2708
D = 128
H, HC = 4, 32
R = 124
T = -(-N // R)
RL = N - (T - 1) * R
PAIRS = T // 2
BW = 2 * R
NB = -(-N // BW)
CAND = 8 * NB
SLOTS = 24
G = 10
E = G * 128
WIDE = 128
PAY = 3
GAP = 256 - BW
EPS = 1e-5
SCALE = float(HC) ** -0.5
NEG = -1.0e30
assert T % 2 == 0 and R < 128 and BW <= 256 and NB + 1 <= 15


class Count:

    def __init__(self, eng, sem, passed=None):
        self.eng, self.sem, self.passed, self.n, self.base = eng, sem, passed, 0, 0

    def did(self, instruction):
        instruction.then_inc(self.sem, 1)
        self.n += 1
        return self.n

    def at(self, mark):
        self.eng.wait_ge(self.sem, self.base + mark)

    def last(self):
        self.at(self.n)

    def at_apart(self, mark):
        self.at(mark)
        self.eng.sem_inc(self.passed)


def outcome(v, order, numerators, denominators, att_read, reads, wg, zx, skip, b, z_ready):
    m = order.did(v.tensor_scalar(b.den[:], denominators, 0.5, None, ALU.max))
    order.at(m)
    m = order.did(v.reciprocal(b.rden[:], b.den[:]))
    order.at(m)
    v.tensor_tensor(b.att[:].rearrange("p (c h) -> p h c", h=H), numerators.rearrange("p (h c) -> p h c", c=HC),
                    b.rden[:].unsqueeze(2).to_broadcast([R, H, HC]), ALU.mult).then_inc(att_read, 1)
    order.eng.wait_ge(att_read, reads)
    m = order.did(v.tensor_tensor_reduce(out=b.tmp[:], in0=b.att[:], in1=wg[:, 0, :], scale=1.0, scalar=0.0,
                                         op0=ALU.mult, op1=ALU.add, accum_out=b.z1[:]))
    order.at(m)
    v.tensor_tensor(b.z2[:], b.z1[:], zx, ALU.add).then_inc(z_ready, 1)
    order.did(v.tensor_tensor(b.diff[:], skip, b.att[:], ALU.subtract))


def mix(v, order, x1, result, b):
    m = order.did(v.tensor_scalar(b.ez[:], b.ez[:], 1.0, None, ALU.add))
    order.at(m)
    m = order.did(v.reciprocal(b.beta[:], b.ez[:]))
    order.at(m)
    m = order.did(v.scalar_tensor_tensor(out=b.tmp[:], in0=b.diff[:], scalar=b.beta[:, 0:1], in1=b.att[:],
                                         op0=ALU.mult, op1=ALU.add))
    order.at(m)
    return order.did(v.tensor_tensor(result, b.tmp[:], x1, ALU.add))


class Gate:

    def __init__(self, sb, ctx, name):
        def rows(part, width):
            return sb(f"{part}_{name}", [R, width], ctx=ctx)

        self.den, self.rden = rows("den", H), rows("rden", H)
        self.att, self.tmp, self.diff = rows("att", D), rows("tmp", D), rows("diff", D)
        self.z1, self.z2, self.ez, self.beta = rows("z1", 1), rows("z2", 1), rows("ez", 1), rows("beta", 1)


def dense_layer0(nc, sb, sem, ps, adj, d_table, s_all, u_all, updT, ident, gl_all):
    with ExitStack() as c:
        dT = sb("dense_dT", [D, T * R], ctx=c)
        sT = sb("dense_sT", [D, T * R], ctx=c)
        aggT = sb("dense_aggT", [D, T * R], ctx=c)
        d_in = sb("dense_d_in", [R, D], ctx=c)
        s_in = sb("dense_s_in", [R, D], ctx=c)
        adj_row = [sb(f"dense_adj{s}", [D, N], ctx=c) for s in range(2)]
        msg = [sb(f"dense_msg{s}", [D, N], ctx=c) for s in range(2)]
        agg = [sb(f"dense_agg{s}", [D, 1], ctx=c) for s in range(2)]
        agg_tile = sb("dense_agg_tile", [D, R], ctx=c)
        cleared = sem("dense_cleared", c)
        d_loaded = sem("dense_d_loaded", c)
        s_copied = sem("dense_s_copied", c)
        turned = sem("dense_turned", c)
        kept = sem("dense_kept", c)
        row_in = [sem(f"dense_row_in{s}", c) for s in range(2)]
        msg_made = sem("dense_msg_made", c)
        agg_made = sem("dense_agg_made", c)
        agg_kept = sem("dense_agg_kept", c)
        tile_copied = sem("dense_tile_copied", c)
        summed = sem("dense_summed", c)
        done = sem("dense_done", c)
        with nc.Block() as block:
            @block.gpsimd
            def _(pool):
                nc.gpsimd.memset(d_in[:], 0.0).then_inc(cleared, 1)
                nc.gpsimd.memset(aggT[:], 0.0).then_inc(cleared, 1)

            @block.sync
            def _(sp):
                sp.wait_ge(cleared, 2)
                sp.dma_start(d_in[:], d_table[0:R, :]).then_inc(d_loaded, 16)
                with sp.Fori(1, T - 1) as t:
                    sp.wait_ge(turned, t)
                    sp.dma_start(d_in[:], d_table[bass.ds(t * R, R), :]).then_inc(d_loaded, 16)
                sp.wait_ge(turned, T - 1)
                sp.dma_start(d_in[0:RL, :], d_table[(T - 1) * R:N, :]).then_inc(d_loaded, 16)
                for s in range(2):
                    sp.dma_start(adj_row[s][:], adj[s:s + 1, :].to_broadcast([D, N])).then_inc(row_in[s], 16)
                with sp.Fori(1, N // 2) as i:
                    for s in range(2):
                        sp.wait_ge(agg_made, 2 * i + s - 1)
                        sp.dma_start(adj_row[s][:], adj[bass.ds(2 * i + s, 1), :].to_broadcast([D, N])).then_inc(
                            row_in[s], 16)

            @block.tensor
            def _(pe):
                pe.wait_ge(d_loaded, 16)
                pe.wait_ge(s_copied, 1)
                nc.tensor.transpose(ps[0][:, 0:R], d_in[:], ident[0:R, 0:R])
                nc.tensor.transpose(ps[0][:, R:2 * R], s_in[:], ident[0:R, 0:R]).then_inc(turned, 1)
                with pe.Fori(1, T) as t:
                    pe.wait_ge(d_loaded, 16 * t + 16)
                    pe.wait_ge(s_copied, t + 1)
                    pe.wait_ge(kept, 2 * t)
                    nc.tensor.transpose(ps[0][:, 0:R], d_in[:], ident[0:R, 0:R])
                    nc.tensor.transpose(ps[0][:, R:2 * R], s_in[:], ident[0:R, 0:R]).then_inc(turned, 1)
                with pe.Fori(0, T) as t:
                    pe.wait_ge(tile_copied, t + 1)
                    nc.tensor.matmul(ps[1][0:R, 0:D], ident[0:R, 0:R], u_all[:, t, :], start=True, stop=False)
                    nc.tensor.matmul(ps[1][0:R, 0:D], agg_tile[:], updT[:], start=False, stop=True).then_inc(summed, 1)

            @block.scalar
            def _(act):
                with act.Fori(0, T) as t:
                    act.wait_ge(turned, t + 1)
                    nc.scalar.copy(dT[:, bass.ds(t * R, R)], ps[0][:, 0:R]).then_inc(kept, 1)
                    nc.scalar.copy(sT[:, bass.ds(t * R, R)], ps[0][:, R:2 * R]).then_inc(kept, 1)
                act.wait_ge(kept, 2 * T)

                def message(n, s):
                    nc.scalar.activation(msg[s][:], dT[:, 0:N], ACT.Gelu, bias=sT[:, bass.ds(n, 1)]).then_inc(
                        msg_made, 1)

                for s in range(2):
                    message(s, s)
                with act.Fori(1, N // 2) as i:
                    for s in range(2):
                        act.wait_ge(agg_made, 2 * i + s - 1)
                        message(2 * i + s, s)
                with act.Fori(0, T) as t:
                    act.wait_ge(summed, t + 1)
                    nc.scalar.activation(gl_all[:, t, :], ps[1][0:R, 0:D], ACT.Gelu).then_inc(done, 1)
                act.wait_ge(done, T)

            @block.vector
            def _(dve):
                v = nc.vector
                v.tensor_copy(s_in[:], s_all[:, 0, :]).then_inc(s_copied, 1)
                with dve.Fori(1, T) as t:
                    dve.wait_ge(turned, t)
                    v.tensor_copy(s_in[:], s_all[:, t, :]).then_inc(s_copied, 1)
                dve.wait_ge(cleared, 2)
                with dve.Fori(0, N // 2) as i:
                    for s in range(2):
                        dve.wait_ge(row_in[s], 16 * i + 16)
                        dve.wait_ge(msg_made, 2 * i + s + 1)
                        v.tensor_tensor_reduce(out=msg[s][:], in0=msg[s][:], in1=adj_row[s][:], scale=1.0,
                                               scalar=0.0, op0=ALU.mult, op1=ALU.add,
                                               accum_out=agg[s][:]).then_inc(agg_made, 1)
                        dve.wait_ge(agg_made, 2 * i + s + 1)
                        v.tensor_copy(aggT[:, bass.ds(2 * i + s, 1)], agg[s][:]).then_inc(agg_kept, 1)
                dve.wait_ge(agg_kept, N)
                v.tensor_copy(agg_tile[:], aggT[:, 0:R]).then_inc(tile_copied, 1)
                with dve.Fori(1, T) as t:
                    dve.wait_ge(done, t)
                    v.tensor_copy(agg_tile[:], aggT[:, bass.ds(t * R, R)]).then_inc(tile_copied, 1)


def dense_layer1(nc, sb, sem, ps, adj, kv_table, qx_all, zx_all, wg, x_all, ident, gl_all):
    COLS = [(a, min(N, a + 512)) for a in range(0, N, 512)]
    with ExitStack() as c:
        kT = sb("dense_kT", [D, T * R], ctx=c)
        V = sb("dense_V", [R, T, D], ctx=c)
        k_in = sb("dense_k_in", [R, D], ctx=c)
        q_in = sb("dense_q_in", [R, D], ctx=c)
        qT = sb("dense_qT", [D, R], ctx=c)
        qh = sb("dense_qh", [D, R], ctx=c)
        of_head = sb("dense_of_head", [D, H], ctx=c)
        adj_t = sb("dense_adj_t", [R, N], ctx=c)
        past = sb("dense_past", [R, N], ctx=c)
        e = sb("dense_e", [R, T * R], ctx=c)
        top = sb("dense_top", [R, 1], ctx=c)
        below = sb("dense_below", [R, 1], ctx=c)
        total = sb("dense_total", [R, 1], ctx=c)
        e_in = sb("dense_e_in", [R, R], ctx=c)
        eT = sb("dense_eT", [R, R], ctx=c)
        num = sb("dense_num", [R, H, HC], ctx=c)
        dens = sb("dense_dens", [R, H], ctx=c)
        gate = Gate(sb, c, "dense")
        made = sem("dense1_made", c)
        k_loaded = sem("dense1_k_loaded", c)
        v_loaded = sem("dense1_v_loaded", c)
        k_turned = sem("dense1_k_turned", c)
        k_kept = sem("dense1_k_kept", c)
        adj_loaded = sem("dense1_adj_loaded", c)
        q_copied = sem("dense1_q_copied", c)
        q_turned = sem("dense1_q_turned", c)
        qT_kept = sem("dense1_qT_kept", c)
        head_ready = sem("dense1_head_ready", c)
        scored = sem("dense1_scored", c)
        scores_read = sem("dense1_scores_read", c)
        below_ready = sem("dense1_below_ready", c)
        exp_done = sem("dense1_exp_done", c)
        e_copied = sem("dense1_e_copied", c)
        e_turned = sem("dense1_e_turned", c)
        eT_kept = sem("dense1_eT_kept", c)
        attended = sem("dense1_attended", c)
        head_done = sem("dense1_head_done", c)
        att_read = sem("dense1_att_read", c)
        z_ready = sem("dense1_z_ready", c)
        ez_ready = sem("dense1_ez_ready", c)
        tile_done = sem("dense1_tile_done", c)
        order_sem = sem("dense1_order", c)
        with nc.Block() as block:
            @block.gpsimd
            def _(pool):
                g = nc.gpsimd
                order = Count(pool, made)
                order.did(g.memset(V[:, T - 1, :], 0.0))
                order.did(g.memset(k_in[:], 0.0))
                order.did(g.memset(e[:, N:T * R], 0.0))
                order.did(g.memset(adj_t[:], 0.0))
                order.did(g.memset(of_head[:], 1.0))
                order.last()
                order.did(g.affine_select(out=of_head[:], in_=of_head[:], compare_op=ALU.is_ge, fill=0.0, base=0,
                                          pattern=[[-HC, H]], channel_multiplier=1))
                order.last()
                order.did(g.affine_select(out=of_head[:], in_=of_head[:], compare_op=ALU.is_ge, fill=0.0,
                                          base=HC - 1, pattern=[[HC, H]], channel_multiplier=-1))

            @block.sync
            def _(sp):
                sp.wait_ge(made, 7)
                v_rows = kv_table[0:(T - 1) * R, D:2 * D].rearrange("(t p) d -> p t d", p=R)
                sp.dma_start(V[:, 0:T - 1, :], v_rows).then_inc(v_loaded, 16)
                sp.dma_start(V[0:RL, T - 1, :], kv_table[(T - 1) * R:N, D:2 * D]).then_inc(v_loaded, 16)
                sp.dma_start(k_in[:], kv_table[0:R, 0:D]).then_inc(k_loaded, 16)
                with sp.Fori(1, T - 1) as t:
                    sp.wait_ge(k_turned, t)
                    sp.dma_start(k_in[:], kv_table[bass.ds(t * R, R), 0:D]).then_inc(k_loaded, 16)
                sp.wait_ge(k_turned, T - 1)
                sp.dma_start(k_in[0:RL, :], kv_table[(T - 1) * R:N, 0:D]).then_inc(k_loaded, 16)
                sp.dma_start(adj_t[:], adj[0:R, :]).then_inc(adj_loaded, 16)
                with sp.Fori(1, T - 1) as t:
                    sp.wait_ge(tile_done, t)
                    sp.dma_start(adj_t[:], adj[bass.ds(t * R, R), :]).then_inc(adj_loaded, 16)
                sp.wait_ge(tile_done, T - 1)
                sp.dma_start(adj_t[0:RL, :], adj[(T - 1) * R:N, :]).then_inc(adj_loaded, 16)
                sp.wait_ge(v_loaded, 32)

            @block.tensor
            def _(pe):
                def turn_k(t):
                    pe.wait_ge(k_loaded, 16 * t + 16)
                    nc.tensor.transpose(ps[0][:, 0:R], k_in[:], ident[0:R, 0:R]).then_inc(k_turned, 1)

                turn_k(0)
                with pe.Fori(1, T) as t:
                    pe.wait_ge(k_kept, t)
                    turn_k(t)
                pe.wait_ge(k_kept, T)
                pe.wait_ge(v_loaded, 32)
                with pe.Fori(0, T) as t:
                    pe.wait_ge(q_copied, t + 1)
                    nc.tensor.transpose(ps[6][:, 0:R], q_in[:], ident[0:R, 0:R]).then_inc(q_turned, 1)
                    with pe.Fori(0, H) as h:
                        pe.wait_ge(head_ready, t * H + h + 1)
                        for n, (a, b) in enumerate(COLS):
                            m = nc.tensor.matmul(ps[n][0:R, 0:b - a], qh[:], kT[:, a:b], start=True, stop=True)
                        m.then_inc(scored, 1)

                        def weigh(j, start):
                            pe.wait_ge(e_copied, (t * H + h) * T + j + 1)
                            nc.tensor.transpose(ps[6][0:R, 0:R], e_in[:], ident[0:R, 0:R]).then_inc(e_turned, 1)
                            pe.wait_ge(eT_kept, (t * H + h) * T + j + 1)
                            nc.tensor.matmul(ps[7][0:R, 0:HC], eT[:], V[:, j, :][:, bass.ds(h * HC, HC)],
                                             start=start, stop=True, skip_group_check=True).then_inc(attended, 1)

                        weigh(0, True)
                        with pe.Fori(1, T) as j:
                            weigh(j, False)

            @block.scalar
            def _(act):
                a_ = nc.scalar
                with act.Fori(0, T) as t:
                    act.wait_ge(k_turned, t + 1)
                    a_.copy(kT[:, bass.ds(t * R, R)], ps[0][:, 0:R]).then_inc(k_kept, 1)
                with act.Fori(0, T) as t:
                    act.wait_ge(q_turned, t + 1)
                    a_.copy(qT[:], ps[6][:, 0:R]).then_inc(qT_kept, 1)
                    with act.Fori(0, H) as h:
                        act.wait_ge(below_ready, t * H + h + 1)
                        a_.activation(e[:, 0:N], e[:, 0:N], ACT.Exp, bias=below[:, 0:1]).then_inc(exp_done, 1)
                        with act.Fori(0, T) as j:
                            act.wait_ge(e_turned, (t * H + h) * T + j + 1)
                            a_.copy(eT[:], ps[6][0:R, 0:R]).then_inc(eT_kept, 1)
                    act.wait_ge(z_ready, t + 1)
                    a_.activation(gate.ez[:], gate.z2[:], ACT.Exp, scale=-1.0).then_inc(ez_ready, 1)

            @block.vector
            def _(dve):
                v = nc.vector
                dve.wait_ge(made, 7)
                order = Count(dve, order_sem)
                PER_HEAD, PER_TILE = 3, 9
                with dve.Fori(0, T) as t:
                    order.base, order.n = dve.snap(t * (PER_TILE + H * PER_HEAD)), 0
                    v.tensor_copy(q_in[:], qx_all[:, t, 0, :]).then_inc(q_copied, 1)
                    dve.wait_ge(adj_loaded, 16 * t + 16)
                    m = order.did(v.tensor_scalar(past[:], adj_t[:], 0.0, NEG, ALU.is_equal, ALU.mult))
                    with dve.Fori(0, H) as h:
                        done = t * H + h + 1
                        dve.wait_ge(qT_kept, t + 1)
                        v.tensor_tensor(qh[:], qT[:], of_head[:, bass.ds(h, 1)].to_broadcast([D, R]),
                                        ALU.mult).then_inc(head_ready, 1)
                        order.at(m)
                        dve.wait_ge(scored, done)
                        for n, (a, b) in enumerate(COLS):
                            v.scalar_tensor_tensor(out=e[:, a:b], in0=ps[n][0:R, 0:b - a], scalar=SCALE,
                                                   in1=past[:, a:b], op0=ALU.mult, op1=ALU.add).then_inc(scores_read, 1)
                        in_head = t * (PER_TILE + H * PER_HEAD) + h * PER_HEAD
                        dve.wait_ge(scores_read, done * len(COLS))
                        v.tensor_reduce(top[:], e[:, 0:N], AX.X, ALU.max).then_inc(order_sem, 1)
                        dve.wait_ge(order_sem, in_head + 2)
                        v.tensor_scalar(below[:], top[:], -1.0, None, ALU.mult).then_inc(below_ready, 1)
                        dve.wait_ge(exp_done, done)
                        v.scalar_tensor_tensor(out=e[:, 0:N], in0=adj_t[:], scalar=0.0, in1=e[:, 0:N],
                                               op0=ALU.not_equal, op1=ALU.mult, accum_out=total[:]).then_inc(order_sem, 1)
                        dve.wait_ge(order_sem, in_head + 3)
                        v.tensor_copy(dens[:, bass.ds(h, 1)], total[:]).then_inc(order_sem, 1)
                        v.tensor_copy(e_in[:], e[:, 0:R]).then_inc(e_copied, 1)
                        with dve.Fori(1, T) as j:
                            dve.wait_ge(attended, (done - 1) * T + j)
                            v.tensor_copy(e_in[:], e[:, bass.ds(j * R, R)]).then_inc(e_copied, 1)
                        dve.wait_ge(attended, done * T)
                        v.tensor_copy(num[:, bass.ds(h, 1), :].rearrange("p a c -> p (a c)"),
                                      ps[7][0:R, 0:HC]).then_inc(head_done, 1)
                    order.n += H * PER_HEAD
                    dve.wait_ge(head_done, t * H + H)
                    order.last()
                    outcome(v, order, num[:].rearrange("p h c -> p (h c)"), dens[:], att_read, t + 1, wg,
                            zx_all[:, bass.ds(t, 1)], qx_all[:, t, 1, :], gate, z_ready)
                    dve.wait_ge(ez_ready, t + 1)
                    order.last()
                    m = mix(v, order, x_all[:, t, :], gl_all[:, t, :], gate)
                    order.at(m)
                    assert order.n == PER_TILE + H * PER_HEAD, order.n
                    dve.sem_inc(tile_done)


def adj_resnorm_kernel(nc, x, adj, msg_w, msg_b, upd_w, upd_b, ln_w, ln_b,
                       Wq, bq, Wk, bk, Wv, bv, Ws, bs, Wb, out, debug=None):
    with ExitStack() as whole:
        def sb(name, shape, dt=F32, ctx=whole):
            return ctx.enter_context(nc.sbuf_tensor(name, shape, dt))

        def sem(name, ctx=whole):
            return ctx.enter_context(nc.semaphore(name))

        d_table = nc.dram_tensor("d_table", (N, D), F32, kind="Internal").ap()
        kv_table = nc.dram_tensor("kv_table", (N, 2 * D), F32, kind="Internal").ap()

        ident = sb("ident", [128, 128])
        ident_bf = sb("ident_bf", [128, 128], BF16)
        before = sb("before", [R, R])
        block_code = sb("block_code", [R, NB, 8], I32)
        slot_f = sb("slot_f", [R, SLOTS])
        rowslot = sb("rowslot", [R, SLOTS])
        group_i = sb("group_i", [R, G], I32)
        lane_i = sb("lane_i", [R, 128 + SLOTS], I32)
        row_number = sb("row_number", [128, 128], BF16)
        slot_of = sb("slot_of", [128, SLOTS], I32)

        x_all = sb("x_all", [R, T, D])
        MT_all = sb("MT_all", [R, T, E], BF16)
        J_all = sb("J_all", [128, T, G], I32)
        RS_all = sb("RS_all", [128, T, G], I32)
        deg_all = sb("deg_all", [R, T])
        bad = sb("bad", [R, 1])
        gl_all = sb("gl_all", [R, T, D])
        w1 = sb("w1", [D, 4, D])
        b1 = sb("b1", [R, 4, D])
        wb = sb("wb", [R, 3, D])
        ln = sb("ln", [R, 2, D])
        eps = sb("eps", [R, 1])
        flag = sb("flag", [1, 1], I32)
        late_in = sem("late_in")

        ps = [whole.enter_context(nc.psum_tensor(f"ps{n}", [128, 512], F32)) for n in range(8)]

        mid = ExitStack()
        whole.enter_context(mid)
        s_all = sb("s_all", [R, T, D], ctx=mid)
        u_all = sb("u_all", [R, T, D], ctx=mid)
        updT = sb("updT", [D, D], ctx=mid)
        with ExitStack() as p0:
            w_in = sb("w_in", [D, 4, D], ctx=p0)
            wT = sb("wT", [D, 3, D], ctx=p0)
            bias0 = sb("bias0", [128, 3, D], ctx=p0)
            xin = [sb(f"xin{s}", [R, D], ctx=p0) for s in range(2)]
            xT = [sb(f"xT{s}", [D, R], ctx=p0) for s in range(2)]
            dst = [sb(f"dst{s}", [R, D], ctx=p0) for s in range(2)]
            const_made = sem("const_made", p0)
            vconst = sem("vconst", p0)
            weights_in = sem("weights_in", p0)
            x_kept = sem("x_kept", p0)
            x_in = [sem(f"x_in{s}", p0) for s in range(2)]
            w_turned = sem("w_turned", p0)
            updT_ready = sem("updT_ready", p0)
            wT_ready = sem("wT_ready", p0)
            x_turned = sem("x_turned", p0)
            xT_ready = sem("xT_ready", p0)
            projected = sem("projected", p0)
            biased = sem("biased", p0)
            d_stored = [sem(f"d_stored{s}", p0) for s in range(2)]
            with nc.Block() as block:
                @block.gpsimd
                def _(pool):
                    g = nc.gpsimd
                    order = Count(pool, const_made)
                    order.did(g.memset(ident[:], 0.0))
                    order.did(g.memset(before[:], 1.0))
                    order.did(g.memset(x_all[:, T - 1, :], 0.0))
                    order.did(g.memset(xin[1][:], 0.0))
                    order.did(g.memset(bad[:], 0.0))
                    order.did(g.memset(eps[:], EPS))
                    order.last()
                    order.did(g.affine_select(out=ident[:], in_=ident[:], compare_op=ALU.not_equal, fill=1.0,
                                              base=0, pattern=[[-1, 128]], channel_multiplier=1))
                    order.did(g.affine_select(out=before[:], in_=before[:], compare_op=ALU.is_gt, fill=0.0,
                                              base=0, pattern=[[1, R]], channel_multiplier=-1))
                    order.did(g.iota(block_code[:], pattern=[[1, NB], [0, 8]], base=1, channel_multiplier=0))
                    order.did(g.iota(slot_f[:], pattern=[[1, SLOTS]], base=0, channel_multiplier=0,
                                     allow_small_or_imprecise_dtypes=True))
                    order.did(g.iota(rowslot[:], pattern=[[128, SLOTS]], base=1, channel_multiplier=1,
                                     allow_small_or_imprecise_dtypes=True))
                    order.did(g.iota(group_i[:], pattern=[[1, G]], base=0, channel_multiplier=0))
                    order.did(g.iota(lane_i[:], pattern=[[1, 128 + SLOTS]], base=128 - SLOTS,
                                     channel_multiplier=0))
                    order.did(g.iota(row_number[:], pattern=[[1, 128]], base=1, channel_multiplier=0,
                                     allow_small_or_imprecise_dtypes=True))
                    order.did(g.iota(slot_of[:], pattern=[[1, SLOTS]], base=0, channel_multiplier=0))
                    made = order.n
                    assert made == 15

                @block.sync
                def _(sp):
                    sp.dma_start(w_in[:, 0:2, :], msg_w.rearrange("o (h d) -> o h d", h=2)).then_inc(weights_in, 16)
                    sp.dma_start(w_in[:, 2:4, :], upd_w.rearrange("o (h d) -> o h d", h=2)).then_inc(weights_in, 16)
                    sp.wait_ge(const_made, 6)
                    x_rows = x[0:(T - 1) * R, :].rearrange("(t p) d -> p t d", p=R)
                    for s in range(2):
                        sp.dma_start(xin[s][:], x[s * R:(s + 1) * R, :]).then_inc(x_in[s], 16)
                    sp.dma_start(bias0[:, 1, :], msg_b[None, :].to_broadcast([128, D])).then_inc(weights_in, 16)
                    sp.dma_start(bias0[:, 2, :], upd_b[None, :].to_broadcast([128, D])).then_inc(weights_in, 16)
                    sp.dma_start(x_all[:, 0:T - 1, :], x_rows).then_inc(x_kept, 16)
                    sp.dma_start(x_all[0:RL, T - 1, :], x[(T - 1) * R:N, :]).then_inc(x_kept, 16)
                    with sp.Fori(1, PAIRS - 1) as i:
                        for s in range(2):
                            sp.wait_ge(x_turned, 2 * i + s - 1)
                            sp.dma_start(xin[s][:], x[bass.ds(i * (2 * R) + s * R, R), :]).then_inc(x_in[s], 16)
                    sp.wait_ge(x_turned, T - 3)
                    sp.dma_start(xin[0][:], x[(T - 2) * R:(T - 1) * R, :]).then_inc(x_in[0], 16)
                    sp.wait_ge(x_turned, T - 2)
                    sp.dma_start(xin[1][0:RL, :], x[(T - 1) * R:N, :]).then_inc(x_in[1], 16)
                    for n, w in enumerate((Wk, Wv, Wq, Ws)):
                        sp.dma_start(w1[:, n, :], w).then_inc(late_in, 16)
                    for n, b in enumerate((bk, bv, bq, bs)):
                        sp.dma_start(b1[:, n, :], b[None, :].to_broadcast([R, D])).then_inc(late_in, 16)
                    for n, b in enumerate((ln_w, ln_b)):
                        sp.dma_start(ln[:, n, :], b[None, :].to_broadcast([R, D])).then_inc(late_in, 16)
                    sp.dma_start(wb[:].rearrange("p a d -> p (a d)"),
                                 Wb.rearrange("d a -> a d").to_broadcast([R, 3 * D])).then_inc(late_in, 16)
                    sp.wait_ge(late_in, 16 * 11)
                    sp.wait_ge(x_kept, 32)

                @block.tensor
                def _(pe):
                    pe.wait_ge(const_made, 15)
                    pe.wait_ge(weights_in, 64)
                    for n, half in enumerate((1, 0, 2, 3)):
                        o = ps[4][:, n * D:(n + 1) * D] if n < 3 else ps[5][:, 0:D]
                        m = nc.tensor.transpose(o, w_in[:, half, :], ident[:])
                    m.then_inc(w_turned, 1)

                    def project(t, s, after):
                        pe.wait_ge(xT_ready, after)
                        if s is not None:
                            nc.tensor.matmul(ps[2 + s][0:R, 0:3 * D], xT[s][:], wT[:].rearrange("d h o -> d (h o)"),
                                             start=True, stop=True).then_inc(projected, 1)

                    def turn(s):
                        nc.tensor.transpose(ps[s][:, 0:R], xin[s][:], ident[0:R, 0:R]).then_inc(x_turned, 1)

                    pe.wait_ge(wT_ready, 1)
                    for s in range(2):
                        pe.wait_ge(x_in[s], 16)
                        turn(s)
                        project(s, s, s + 1)
                    with pe.Fori(1, PAIRS) as i:
                        for s in range(2):
                            pe.wait_ge(x_in[s], 16 * i + 16)
                            turn(s)
                            pe.wait_ge(biased, 2 * i + s - 1)
                            project(2 * i + s, s, 2 * i + s + 1)

                @block.scalar
                def _(act):
                    act.wait_ge(const_made, 15)
                    nc.scalar.copy(ident_bf[:], ident[:]).then_inc(updT_ready, 1)
                    act.wait_ge(w_turned, 1)
                    nc.scalar.copy(updT[:], ps[5][:, 0:D]).then_inc(updT_ready, 1)

                    def take(s, t1):
                        act.wait_ge(x_turned, t1)
                        nc.scalar.copy(xT[s][:], ps[s][:, 0:R]).then_inc(xT_ready, 1)

                    for s in range(2):
                        take(s, s + 1)
                    with act.Fori(1, PAIRS) as i:
                        for s in range(2):
                            act.wait_ge(projected, 2 * i + s - 1)
                            take(s, 2 * i + s + 1)

                @block.vector
                def _(dve):
                    v = nc.vector
                    dve.wait_ge(const_made, 15)
                    order = Count(dve, vconst)
                    order.did(v.memset(bias0[:, 0, :], 0.0))
                    order.did(v.tensor_scalar(block_code[:], block_code[:], 27, None, ALU.logical_shift_left))
                    order.did(v.tensor_scalar(lane_i[:], lane_i[:], 127, None, ALU.bitwise_and))
                    order.last()
                    dve.wait_ge(w_turned, 1)
                    v.tensor_copy(wT[:].rearrange("d h o -> d (h o)"), ps[4][:, 0:3 * D]).then_inc(wT_ready, 1)
                    dve.wait_ge(weights_in, 64)

                    def add_bias(t, s, after):
                        dve.wait_ge(projected, after)
                        v.tensor_copy(dst[s][:], ps[2 + s][0:R, 0:D])
                        v.tensor_tensor(s_all[:, t, :], ps[2 + s][0:R, D:2 * D], bias0[0:R, 1, :], ALU.add)
                        v.tensor_tensor(u_all[:, t, :], ps[2 + s][0:R, 2 * D:3 * D], bias0[0:R, 2, :],
                                        ALU.add).then_inc(biased, 1)

                    for s in range(2):
                        add_bias(s, s, s + 1)
                    with dve.Fori(1, PAIRS) as i:
                        for s in range(2):
                            dve.wait_ge(d_stored[s], 16 * i)
                            add_bias(i * 2 + s, s, 2 * i + s + 1)
                    dve.wait_ge(biased, T)

                @block.gpsimd
                def _(pool):
                    def store(rows, s, after, count=R):
                        pool.wait_ge(biased, after)
                        pool.dma_start(rows, dst[s][0:count, :]).then_inc(d_stored[s], 16)

                    with pool.Fori(0, PAIRS - 1) as i:
                        for s in range(2):
                            store(d_table[bass.ds(i * (2 * R) + s * R, R), :], s, 2 * i + s + 1)
                    store(d_table[(T - 2) * R:(T - 1) * R, :], 0, T - 1)
                    store(d_table[(T - 1) * R:N, :], 1, T, RL)
                    for s in range(2):
                        pool.wait_ge(d_stored[s], 16 * PAIRS)

        with ExitStack() as p1:
            adj_t = [sb(f"adj{s}", [R, N], ctx=p1) for s in range(2)]
            sgn = sb("sgn", [R, N], BF16, ctx=p1)
            nz = [sb(f"nz{s}", [R, 1], ctx=p1) for s in range(2)]
            cw = sb("cw", [R, CAND], ctx=p1)
            ci = sb("ci", [R, CAND], U32, ctx=p1)
            code = sb("code", [R, CAND], I32, ctx=p1)
            keys = [sb(f"keys{n}", [R, CAND], ctx=p1) for n in range(2)]
            keys_b = [sb(f"keys_b{n}", [R, CAND], ctx=p1) for n in range(2)]
            best = [sb(f"best{n}", [R, SLOTS], ctx=p1) for n in range(2)]
            valid = sb("valid", [R, SLOTS], ctx=p1)
            deg = sb("deg", [R, WIDE], ctx=p1)
            jcode = sb("jcode", [R, SLOTS], I32, ctx=p1)
            blk = sb("blk", [R, SLOTS], I32, ctx=p1)
            node = sb("node", [128, G], ctx=p1)
            whigh = sb("whigh", [R, SLOTS], I32, ctx=p1)
            pay = sb("pay", [R, SLOTS, PAY], ctx=p1)
            off = sb("off", [R, 1], ctx=p1)
            end = sb("end", [R, 1], ctx=p1)
            pos = sb("pos", [R, SLOTS], I32, ctx=p1)
            grp = sb("grp", [R, SLOTS], I32, ctx=p1)
            lane = sb("lane", [R, 1], I32, ctx=p1)
            lane_hot = sb("lane_hot", [R, 128 + SLOTS], ctx=p1)
            grp_hot = sb("grp_hot", [R, SLOTS, G], ctx=p1)
            rhs = sb("rhs", [R, SLOTS * G * PAY + WIDE], ctx=p1)
            rhs_slots = rhs[:, 0:SLOTS * G * PAY].rearrange("p (k g a) -> p k g a", k=SLOTS, g=G)
            J = [sb(f"J{s}", [128, G], I32, ctx=p1) for s in range(2)]
            RS = [sb(f"RS{s}", [128, G], I32, ctx=p1) for s in range(2)]
            row_i = sb("row_i", [128, G], I32, ctx=p1)
            row_b = sb("row_b", [128, G], BF16, ctx=p1)
            w_e = [sb(f"w_e{s}", [128, G], ctx=p1) for s in range(2)]
            M = [sb(f"M{s}", [128, G, 128], BF16, ctx=p1) for s in range(2)]
            Mw = [sb(f"Mw{s}", [128, G, 128], ctx=p1) for s in range(2)]
            MT = [sb(f"MT{s}", [R, E], ctx=p1) for s in range(2)]
            gath = [sb(f"gath{s}", [128, G, D], ctx=p1) for s in range(2)]
            msg = sb("msg", [128, G, D], ctx=p1)
            aggT = sb("aggT", [D, R], ctx=p1)

            adj_loaded = [sem(f"adj_loaded{s}", p1) for s in range(2)]
            adj_scanned = sem("adj_scanned", p1)
            adj_counted = sem("adj_counted", p1)
            deg_ready = sem("deg_ready", p1)
            filled = sem("filled", p1)
            off_ready = sem("off_ready", p1)
            slots_ready = sem("slots_ready", p1)
            packed = sem("packed", p1)
            index_ready = sem("index_ready", p1)
            lists_kept = sem("lists_kept", p1)
            hot_ready = sem("hot_ready", p1)
            mw_ready = sem("mw_ready", p1)
            hot_turned = sem("hot_turned", p1)
            MT_ready = sem("MT_ready", p1)
            gathered = [sem(f"gathered{s}", p1) for s in range(2)]
            sums_ready = sem("sums_ready", p1)
            msg_ready = sem("msg_ready", p1)
            agg_ready = sem("agg_ready", p1)
            aggT_ready = sem("aggT_ready", p1)
            upd_ready = sem("upd_ready", p1)
            gl_ready = sem("gl_ready", p1)
            dve_order = sem("dve_order", p1)
            dve_passed = sem("dve_passed", p1)
            pool_passed = sem("pool_passed", p1)
            act_order = sem("act_order", p1)

            ps_msg = ps[0:3]
            ps_turn = [ps[n][:].bitcast(BF16) for n in (3, 4)]
            ps_off, ps_pack = ps[7][0:R, 0:WIDE], ps[5][:, 0:WIDE]
            ps_agg, ps_upd = ps[6][:, 0:R], ps[6][0:R, 128:128 + D]
            CHUNKS = [(0, 4), (4, 8), (8, G)]

            with nc.Block() as block:
                @block.sync
                def _(sp):
                    for s in range(2):
                        sp.dma_start(adj_t[s][:], adj[s * R:(s + 1) * R, :]).then_inc(adj_loaded[s], 16)
                    with sp.Fori(1, PAIRS - 1) as i:
                        for s in range(2):
                            sp.wait_ge(adj_scanned, 2 * i + s - 1)
                            sp.wait_ge(adj_counted, 2 * i + s - 1)
                            sp.dma_start(adj_t[s][:], adj[bass.ds(i * (2 * R) + s * R, R), :]).then_inc(
                                adj_loaded[s], 16)
                    sp.wait_ge(adj_scanned, T - 3)
                    sp.wait_ge(adj_counted, T - 3)
                    sp.dma_start(adj_t[0][:], adj[(T - 2) * R:(T - 1) * R, :]).then_inc(adj_loaded[0], 16)
                    sp.wait_ge(adj_scanned, T - 2)
                    sp.wait_ge(adj_counted, T - 2)
                    sp.dma_start(adj_t[1][0:RL, :], adj[(T - 1) * R:N, :]).then_inc(adj_loaded[1], 16)

                @block.gpsimd
                def _(pool):
                    def gather(t, s, i, first):
                        pool.wait_ge(index_ready, t + 1)
                        if not first:
                            pool.wait_ge(sums_ready, 3 * t - 3)
                        pool.sem_inc(pool_passed)
                        for g in range(G):
                            pool.indirect_dma_start(
                                out=gath[s][:, g, :], out_offset=None, in_=d_table,
                                in_offset=bass.IndirectOffsetOnAxis(ap=J[s][:, g:g + 1], axis=0),
                            ).then_inc(gathered[s], 16)
                        pool.wait_ge(hot_ready, t + 1)
                        if not first:
                            pool.wait_ge(agg_ready, t - 1)
                        nc.gpsimd.tensor_tensor(Mw[s][:], M[s][:], w_e[s][:].unsqueeze(2).to_broadcast([128, G, 128]),
                                                ALU.mult).then_inc(mw_ready, 1)
                        nc.gpsimd.tensor_copy(J_all[:, t, :], J[s][:]).then_inc(lists_kept, 1)
                        nc.gpsimd.tensor_copy(RS_all[:, t, :], RS[s][:]).then_inc(lists_kept, 1)

                    nc.gpsimd.memset(deg[:], 0.0).then_inc(filled, 1)
                    nc.gpsimd.memset(rhs[:, SLOTS * G * PAY:], 0.0).then_inc(filled, 1)
                    for s in range(2):
                        gather(s, s, 0, True)
                    with pool.Fori(1, PAIRS) as i:
                        for s in range(2):
                            gather(2 * i + s, s, i, False)
                    pool.wait_ge(lists_kept, 2 * T)

                @block.vector
                def _(dve):
                    v = nc.vector
                    order = Count(dve, dve_order, dve_passed)

                    def scan_weights(t, s, i):
                        dve.wait_ge(adj_loaded[s], 16 * i + 16)
                        dve.sem_inc(dve_passed)
                        for b in range(NB):
                            order.did(v.max(out=cw[:, 8 * b:8 * b + 8], in_=adj_t[s][:, b * BW:min(N, (b + 1) * BW)]))

                    def scan_columns(t, s):
                        order.at_apart(order.n)
                        for b in range(NB):
                            m = v.max_index(out=ci[:, 8 * b:8 * b + 8], in_max=cw[:, 8 * b:8 * b + 8],
                                            in_values=adj_t[s][:, b * BW:min(N, (b + 1) * BW)])
                            if b < NB - 1:
                                order.did(m)
                        m.then_inc(adj_scanned, 1)

                    def slots(t, s):
                        bits = cw[:].bitcast(I32)
                        flat = block_code[:].rearrange("p b e -> p (b e)")
                        dve.wait_ge(adj_scanned, t + 1)
                        m = order.did(v.scalar_tensor_tensor(out=code[:], in0=ci[:].bitcast(I32), scalar=19, in1=flat,
                                                             op0=ALU.logical_shift_left, op1=ALU.bitwise_or))
                        order.at(m)
                        order.did(v.scalar_tensor_tensor(out=keys_b[0][:].bitcast(I32), in0=bits, scalar=12,
                                                         in1=code[:], op0=ALU.logical_shift_right,
                                                         op1=ALU.bitwise_or))
                        m = order.did(v.scalar_tensor_tensor(out=keys_b[1][:].bitcast(I32), in0=bits, scalar=0xFFF,
                                                             in1=code[:], op0=ALU.bitwise_and, op1=ALU.bitwise_or))
                        for n in range(2):
                            order.at(m - 1 + n)
                            m2 = order.did(v.scalar_tensor_tensor(out=keys[n][:], in0=cw[:], scalar=0.0,
                                                                  in1=keys_b[n][:], op0=ALU.is_gt, op1=ALU.mult))
                        for r in range(SLOTS // 8):
                            src = keys if r % 2 == 0 else keys_b
                            dst_ = keys_b if r % 2 == 0 else keys
                            for n in range(2):
                                order.at_apart(m2 - 1 + n)
                                m3 = order.did(v.max(out=best[n][:, 8 * r:8 * r + 8], in_=src[n][:]))
                            m2 = m3
                            if r < SLOTS // 8 - 1:
                                for n in range(2):
                                    order.at_apart(m3 - 1 + n)
                                    m2 = order.did(v.match_replace(out=dst_[n][:], in_to_replace=best[n][:, 8 * r:8 * r + 8],
                                                                   in_values=src[n][:], imm_value=0.0))
                        order.at(m2 - 1)
                        order.did(v.tensor_scalar(valid[:], best[0][:], 0.0, 0.0, ALU.is_gt, ALU.add,
                                                  accum_out=deg[:, 0:1]))
                        order.did(v.tensor_scalar(jcode[:], best[0][:].bitcast(I32), 19, None,
                                                  ALU.logical_shift_right))
                        order.did(v.tensor_scalar(blk[:], best[0][:].bitcast(I32), 27, None,
                                                  ALU.logical_shift_right))
                        m = order.did(v.tensor_scalar(whigh[:], best[0][:].bitcast(I32), 0x7FFFF, 12,
                                                      ALU.bitwise_and, ALU.logical_shift_left))
                        order.at(m)
                        order.did(v.scalar_tensor_tensor(out=pay[:, :, 2].bitcast(I32), in0=best[1][:].bitcast(I32),
                                                         scalar=0xFFF, in1=whigh[:], op0=ALU.bitwise_and,
                                                         op1=ALU.bitwise_or))
                        order.did(v.scalar_tensor_tensor(out=pay[:, :, 0], in0=blk[:], scalar=float(-GAP),
                                                         in1=jcode[:], op0=ALU.mult, op1=ALU.add))
                        order.did(v.tensor_copy(deg_all[:, bass.ds(t, 1)], deg[:, 0:1]))
                        v.tensor_tensor(pay[:, :, 1], valid[:], rowslot[:], ALU.mult).then_inc(deg_ready, 1)

                    def place(t, s):
                        dve.wait_ge(off_ready, t + 1)
                        dve.wait_ge(adj_counted, t + 1)
                        m = order.did(v.tensor_copy(off[:], ps_off[:, 0:1]))
                        order.at(m)
                        order.did(v.tensor_copy(lane[:], off[:]))
                        order.did(v.tensor_scalar(pos[:], slot_f[:], off[:, 0:1], None, ALU.add))
                        order.did(v.tensor_tensor(end[:], off[:], deg[:, 0:1], ALU.add))
                        order.did(v.scalar_tensor_tensor(out=bad[:], in0=deg[:, 0:1], scalar=nz[s][:, 0:1], in1=bad[:],
                                                         op0=ALU.not_equal, op1=ALU.max))
                        order.at(order.n - 3)
                        order.did(v.tensor_scalar(lane[:], lane[:], 127, None, ALU.bitwise_and))
                        order.at(order.n - 3)
                        order.did(v.tensor_scalar(grp[:], pos[:], 7, None, ALU.logical_shift_right))
                        order.at(order.n - 2)
                        order.did(v.scalar_tensor_tensor(out=bad[:], in0=end[:], scalar=float(E), in1=bad[:],
                                                         op0=ALU.is_gt, op1=ALU.max))
                        order.at(order.n - 1)
                        order.did(v.tensor_tensor(grp_hot[:], grp[:].unsqueeze(2).to_broadcast([R, SLOTS, G]),
                                                  group_i[:].unsqueeze(1).to_broadcast([R, SLOTS, G]), ALU.is_equal))
                        order.did(v.tensor_tensor(lane_hot[:], lane_i[:], lane[:].to_broadcast([R, 128 + SLOTS]),
                                                  ALU.is_equal))
                        order.at(order.n - 1)
                        v.tensor_tensor(rhs_slots, grp_hot[:].unsqueeze(3).to_broadcast([R, SLOTS, G, PAY]),
                                        pay[:].unsqueeze(2).to_broadcast([R, SLOTS, G, PAY]),
                                        ALU.mult).then_inc(slots_ready, 1)

                    def edges(t, s, first):
                        dve.wait_ge(packed, t + 1)
                        if not first:
                            dve.wait_ge(lists_kept, 2 * t - 2)
                            dve.wait_ge(mw_ready, t - 1)
                            dve.wait_ge(hot_turned, t - 1)
                        pk = ps_pack[:, 0:G * PAY].rearrange("p (g a) -> p g a", a=PAY)
                        m = order.did(v.tensor_scalar(node[:], pk[:, :, 0], float(BW), float(BW + N - 1),
                                                      ALU.max, ALU.min))
                        m_rs = order.did(v.tensor_copy(RS[s][:], pk[:, :, 1]))
                        order.at(m)
                        v.tensor_scalar(J[s][:], node[:], float(BW), None, ALU.subtract).then_inc(index_ready, 1)
                        order.at(m_rs)
                        m = order.did(v.tensor_scalar(row_i[:], RS[s][:], 127, None, ALU.bitwise_and))
                        order.did(v.tensor_copy(w_e[s][:], pk[:, :, 2]))
                        order.at(m)
                        m = order.did(v.tensor_copy(row_b[:], row_i[:]))
                        order.at(m)
                        v.tensor_tensor(M[s][:], row_number[:].unsqueeze(1).to_broadcast([128, G, 128]),
                                        row_b[:].unsqueeze(2).to_broadcast([128, G, 128]),
                                        ALU.is_equal).then_inc(hot_ready, 1)

                    def step(t, s, i, now=True, prev=True, first=False):
                        if now:
                            scan_weights(t, s, i)
                        if prev:
                            place(t - 1, 1 - s)
                        if now:
                            scan_columns(t, s)
                        if now:
                            slots(t, s)
                        if prev:
                            edges(t - 1, 1 - s, first)

                    dve.wait_ge(filled, 2)
                    step(0, 0, 0, prev=False)
                    step(1, 1, 0, first=True)
                    a = order.n
                    step(2, 0, 1, first=True)
                    step(3, 1, 1)
                    start = order.n
                    per_pair = start - a
                    with dve.Fori(2, PAIRS) as i:
                        order.base = dve.snap(i * per_pair - 2 * per_pair + start)
                        order.n = 0
                        for s in range(2):
                            step(2 * i + s, s, i)
                        assert order.n == per_pair
                    order.base, order.n = 0, start + (PAIRS - 2) * per_pair
                    step(T, 0, PAIRS, now=False)

                @block.tensor
                def _(pe):
                    mm, tr = nc.tensor.matmul, nc.tensor.transpose

                    def pack(t):
                        pe.wait_ge(slots_ready, t + 1)
                        for k in range(SLOTS):
                            m = mm(ps_pack, lane_hot[:, SLOTS - k:SLOTS - k + 128],
                                   rhs[:, k * G * PAY:k * G * PAY + WIDE],
                                   start=(k == 0), stop=(k == SLOTS - 1))
                        m.then_inc(packed, 1)

                    def turn(t, s, first):
                        pe.wait_ge(hot_ready, t + 1)
                        if not first:
                            pe.wait_ge(MT_ready, 4 * t)
                        for g in range(G):
                            m = tr(ps_turn[g // 8][:, (g % 8) * 128:(g % 8 + 1) * 128], M[s][:, g, :], ident_bf[:])
                        m.then_inc(hot_turned, 1)

                    def offsets(t):
                        pe.wait_ge(deg_ready, t + 1)
                        mm(ps_off, before[:], deg[:], start=True, stop=True).then_inc(off_ready, 1)

                    def messages(t, s, i, first):
                        pe.wait_ge(MT_ready, 4 * t + 4)
                        pe.wait_ge(gathered[s], 16 * G * (i + 1))
                        for c, (a, b) in enumerate(CHUNKS):
                            if not first:
                                pe.wait_ge(msg_ready, 3 * t + c - 2)
                            for g in range(a, b):
                                o = ps_msg[c][:, (g - a) * D:(g - a + 1) * D]
                                mm(o, MT[s][:, g * 128:(g + 1) * 128], s_all[:, t, :], start=True, stop=False)
                                m = mm(o, ident[:], gath[s][:, g, :], start=False, stop=True)
                            m.then_inc(sums_ready, 1)
                        pe.wait_ge(mw_ready, t + 1)
                        if not first:
                            pe.wait_ge(gl_ready, t)
                        for c, (a, b) in enumerate(CHUNKS):
                            pe.wait_ge(msg_ready, 3 * t + c + 1)
                            for g in range(a, b):
                                m = mm(ps_agg, msg[:, g, :], Mw[s][:, g, 0:R], start=(g == 0), stop=(g == G - 1))
                        m.then_inc(agg_ready, 1)

                    def update(t, first):
                        pe.wait_ge(aggT_ready, t + 1)
                        mm(ps_upd, ident[0:R, 0:R], u_all[:, t, :], start=True, stop=False)
                        mm(ps_upd, aggT[:], updT[:], start=False, stop=True).then_inc(upd_ready, 1)

                    def step(t, s, i, now=True, prev=True, prev2=True, first1=False, first2=False):
                        if prev:
                            pack(t - 1)
                        if now:
                            offsets(t)
                        if prev2:
                            messages(t - 2, s, i - 1, first2)
                            update(t - 2, first2)
                        if prev:
                            turn(t - 1, 1 - s, first1)

                    step(0, 0, 0, prev=False, prev2=False)
                    step(1, 1, 0, prev2=False, first1=True)
                    step(2, 0, 1, first2=True)
                    step(3, 1, 1)
                    with pe.Fori(2, PAIRS) as i:
                        for s in range(2):
                            step(2 * i + s, s, i)
                    step(T, 0, PAIRS, now=False)
                    step(T + 1, 1, PAIRS, now=False, prev=False)

                @block.scalar
                def _(act):
                    a = nc.scalar

                    def gelus(t, s, first):
                        for c, (lo, hi) in enumerate(CHUNKS):
                            act.wait_ge(sums_ready, 3 * t + c + 1)
                            if not first:
                                act.wait_ge(agg_ready, t)
                            a.activation(msg[:, lo:hi, :].rearrange("p g d -> p (g d)"),
                                         ps_msg[c][:, 0:(hi - lo) * D], ACT.Gelu).then_inc(msg_ready, 1)
                        act.wait_ge(agg_ready, t + 1)
                        if not first:
                            act.wait_ge(upd_ready, t)
                        a.copy(aggT[:], ps_agg).then_inc(aggT_ready, 1)
                        act.wait_ge(upd_ready, t + 1)
                        a.activation(gl_all[:, t, :], ps_upd, ACT.Gelu).then_inc(gl_ready, 1)

                    def take_turned(t, s, first):
                        act.wait_ge(hot_turned, t + 1)
                        if not first:
                            act.wait_ge(sums_ready, 3 * t - 3)
                        for n, (lo, hi) in enumerate(((0, 1024), (1024, E))):
                            a.copy(MT[s][:, lo:hi], ps_turn[n][0:R, 0:hi - lo]).then_inc(MT_ready, 1)
                            a.copy(MT_all[:, t, lo:hi], ps_turn[n][0:R, 0:hi - lo]).then_inc(MT_ready, 1)

                    def count(t, s, i, first):
                        act.wait_ge(adj_loaded[s], 16 * i + 16)
                        if not first:
                            act.wait_ge(act_order, 2 * t)
                            act.wait_ge(slots_ready, t - 1)
                        a.activation(sgn[:], adj_t[s][:], ACT.Sign).then_inc(act_order, 1)
                        act.wait_ge(act_order, 2 * t + 1)
                        a.activation(sgn[:], sgn[:], ACT.Square, accum_out=nz[s][:]).then_inc(adj_counted, 1)
                        act.wait_ge(adj_counted, t + 1)
                        a.sem_inc(act_order, 1)

                    def step(t, s, i, now=True, prev=True, prev2=True, first0=False, first1=False, first2=False):
                        if now:
                            count(t, s, i, first0)
                        if prev2:
                            gelus(t - 2, s, first2)
                        if prev:
                            take_turned(t - 1, 1 - s, first1)

                    step(0, 0, 0, prev=False, prev2=False, first0=True)
                    step(1, 1, 0, prev2=False, first0=True, first1=True)
                    step(2, 0, 1, first1=True, first2=True)
                    step(3, 1, 1)
                    with act.Fori(2, PAIRS) as i:
                        for s in range(2):
                            step(2 * i + s, s, i)
                    step(T, 0, PAIRS, now=False)
                    step(T + 1, 1, PAIRS, now=False, prev=False)
                    act.wait_ge(gl_ready, T)


        with ExitStack() as pf:
            bad_turned = sem("bad_turned", pf)
            flag_ready = sem("flag_ready", pf)
            with nc.Block() as block:
                @block.tensor
                def _(pe):
                    nc.tensor.transpose(ps[0][0:1, 0:R], bad[:], ident[0:R, 0:R]).then_inc(bad_turned, 1)

                @block.vector
                def _(dve):
                    dve.wait_ge(bad_turned, 1)
                    nc.vector.tensor_reduce(flag[:], ps[0][0:1, 0:R], AX.X, ALU.max).then_inc(flag_ready, 1)
                    dve.wait_ge(flag_ready, 1)

        with nc.If(nc.values_load(flag[0:1, 0:1], min_val=0, max_val=1)):
            dense_layer0(nc, sb, sem, ps, adj, d_table, s_all, u_all, updT, ident, gl_all)
        mid.close()

        qx_all = sb("qx_all", [R, T, 2, D])
        zx_all = sb("zx_all", [R, T])
        wg = sb("wg", [R, 2, D])
        HALVES = [(0, T // 2), (T // 2, T)]

        def normed(v, order, h, stats, a, b, centred, squared, std_ready, n, sq):
            mean, var, rstd = stats[0][:, a:b], stats[1][:, a:b], stats[2][:, a:b]
            m = order.did(v.tensor_reduce(mean, h[:, a:b, :], AX.X, ALU.add))
            order.at(m)
            m = order.did(v.tensor_scalar(mean, mean, 1.0 / D, None, ALU.mult))
            order.at(m)
            v.tensor_tensor(h[:, a:b, :], h[:, a:b, :], mean.unsqueeze(2).to_broadcast([R, b - a, D]),
                            ALU.subtract).then_inc(centred, 1)

        def deviation(v, dve, order, stats, a, b, squared, var_ready, n, sq):
            dve.wait_ge(squared, n)
            v.tensor_reduce(stats[1][:, a:b], sq[:, a:b, :], AX.X, ALU.add).then_inc(var_ready, 1)

        def inverse(v, dve, order, stats, a, b, std_ready, n):
            dve.wait_ge(std_ready, n)
            m = order.did(v.reciprocal(stats[2][:, a:b], stats[1][:, a:b]))
            order.at(m)

        def scalar_norm(a_, act, h, stats, centred, squared, var_ready, std_ready, sq, n0):
            for n, (a, b) in enumerate(HALVES):
                act.wait_ge(centred, n0 + n + 1)
                a_.activation(sq[:, a:b, :], h[:, a:b, :], ACT.Square).then_inc(squared, 1)
            for n, (a, b) in enumerate(HALVES):
                act.wait_ge(var_ready, n0 + n + 1)
                a_.activation(stats[1][:, a:b], stats[1][:, a:b], ACT.Sqrt, scale=1.0 / D,
                              bias=eps[:, 0:1]).then_inc(std_ready, 1)

        with ExitStack() as pm:
            sq = sb("sq", [R, T, D], ctx=pm)
            stats = [sb(f"stats{n}", [R, T], ctx=pm) for n in range(3)]
            x1 = [sb(f"x1_{s}", [R, D], ctx=pm) for s in range(2)]
            x1T = [sb(f"x1T{s}", [D, R], ctx=pm) for s in range(2)]
            kvs = [sb(f"kvs{s}", [R, 2 * D], ctx=pm) for s in range(2)]
            m_order = sem("m_order", pm)
            centred = sem("centred", pm)
            squared = sem("squared", pm)
            var_ready = sem("var_ready", pm)
            std_ready = sem("std_ready", pm)
            x1_ready = sem("x1_ready", pm)
            x1_turned = sem("x1_turned", pm)
            x1T_ready = sem("x1T_ready", pm)
            x1_kept = sem("x1_kept", pm)
            proj1 = sem("proj1", pm)
            kv_ready = sem("kv_ready", pm)
            qx_ready = sem("qx_ready", pm)
            kv_stored = [sem(f"kv_stored{s}", pm) for s in range(2)]
            with nc.Block() as block:
                @block.vector
                def _(dve):
                    v = nc.vector
                    order = Count(dve, m_order)
                    order.did(v.tensor_tensor(wg[:, 0, :], wb[:, 0, :], wb[:, 2, :], ALU.add))
                    order.did(v.tensor_tensor(wg[:, 1, :], wb[:, 1, :], wb[:, 2, :], ALU.subtract))
                    for n, (a, b) in enumerate(HALVES):
                        m = order.did(v.tensor_tensor(gl_all[:, a:b, :], gl_all[:, a:b, :], x_all[:, a:b, :], ALU.add))
                        order.at(m)
                        normed(v, order, gl_all, stats, a, b, centred, squared, std_ready, n, sq)
                    for n, (a, b) in enumerate(HALVES):
                        deviation(v, dve, order, stats, a, b, squared, var_ready, n + 1, sq)
                    for n, (a, b) in enumerate(HALVES):
                        inverse(v, dve, order, stats, a, b, std_ready, n + 1)
                        part, shape = gl_all[:, a:b, :], [R, b - a, D]
                        for in1, op in ((stats[2][:, a:b].unsqueeze(2), ALU.mult), (ln[:, 0:1, :], ALU.mult),
                                        (ln[:, 1:2, :], ALU.add), (x_all[:, a:b, :], ALU.add)):
                            m = order.did(v.tensor_tensor(part, part, in1.to_broadcast(shape), op))
                            order.at(m)
                        normed(v, order, gl_all, stats, a, b, centred, squared, std_ready, n + 2, sq)
                    for n, (a, b) in enumerate(HALVES):
                        deviation(v, dve, order, stats, a, b, squared, var_ready, n + 3, sq)
                    for n, (a, b) in enumerate(HALVES):
                        inverse(v, dve, order, stats, a, b, std_ready, n + 3)

                    def norm(t, s, first):
                        if not first:
                            dve.wait_ge(x1_kept, t - 1)
                        v.tensor_tensor(x1[s][:], gl_all[:, t, :], stats[2][:, bass.ds(t, 1)].to_broadcast([R, D]),
                                        ALU.mult).then_inc(x1_ready, 1)

                    def add_bias(t, s, stored):
                        dve.wait_ge(proj1, t + 1)
                        if stored is not None:
                            dve.wait_ge(kv_stored[s], stored)
                        v.tensor_tensor(kvs[s][:], ps[2 + s][0:R, 0:2 * D],
                                        b1[:, 0:2, :].rearrange("p a d -> p (a d)"), ALU.add).then_inc(kv_ready, 1)
                        v.tensor_tensor(qx_all[:, t, :, :].rearrange("p a d -> p (a d)"), ps[2 + s][0:R, 2 * D:4 * D],
                                        b1[:, 2:4, :].rearrange("p a d -> p (a d)"), ALU.add).then_inc(qx_ready, 1)

                    norm(0, 0, True)
                    norm(1, 1, True)
                    add_bias(0, 0, None)
                    norm(2, 0, False)
                    add_bias(1, 1, None)
                    with dve.Fori(1, PAIRS - 1) as i:
                        norm(2 * i + 1, 1, False)
                        add_bias(2 * i, 0, 16 * i)
                        norm(2 * i + 2, 0, False)
                        add_bias(2 * i + 1, 1, 16 * i)
                    norm(T - 1, 1, False)
                    add_bias(T - 2, 0, 16 * (PAIRS - 1))
                    add_bias(T - 1, 1, 16 * (PAIRS - 1))
                    dve.wait_ge(qx_ready, T)
                    m = order.did(v.tensor_tensor(sq[:], qx_all[:, :, 1, :], wg[:, 1:2, :].to_broadcast([R, T, D]),
                                                  ALU.mult))
                    order.at(m)
                    m = order.did(v.tensor_reduce(zx_all[:], sq[:], AX.X, ALU.add))
                    order.at(m)

                @block.scalar
                def _(act):
                    a = nc.scalar
                    scalar_norm(a, act, gl_all, stats, centred, squared, var_ready, std_ready, sq, 0)
                    scalar_norm(a, act, gl_all, stats, centred, squared, var_ready, std_ready, sq, 2)

                    def take(t, s, first):
                        act.wait_ge(x1_ready, t + 1)
                        if first:
                            act.wait_ge(x1_turned, t + 1)
                        else:
                            act.wait_ge(x1_turned, t + 1)
                            act.wait_ge(proj1, t - 1)
                        a.copy(x1T[s][:], ps[s][:, 0:R]).then_inc(x1T_ready, 1)
                        a.copy(x_all[:, t, :], x1[s][:]).then_inc(x1_kept, 1)

                    for s in range(2):
                        take(s, s, True)
                    with act.Fori(1, PAIRS) as i:
                        for s in range(2):
                            take(2 * i + s, s, False)
                    act.wait_ge(x1_kept, T)

                @block.tensor
                def _(pe):
                    def project(t, s, first):
                        pe.wait_ge(x1_ready, t + 1)
                        nc.tensor.transpose(ps[s][:, 0:R], x1[s][:], ident[0:R, 0:R]).then_inc(x1_turned, 1)
                        pe.wait_ge(x1T_ready, t + 1)
                        if not first:
                            pe.wait_ge(qx_ready, t - 1)
                        nc.tensor.matmul(ps[2 + s][0:R, :], x1T[s][:], w1[:].rearrange("p a d -> p (a d)"),
                                         start=True, stop=True).then_inc(proj1, 1)

                    for s in range(2):
                        project(s, s, True)
                    with pe.Fori(1, PAIRS) as i:
                        for s in range(2):
                            project(2 * i + s, s, False)

                @block.sync
                def _(sp):
                    def store(rows, t, s, count=R):
                        sp.wait_ge(kv_ready, t + 1)
                        sp.dma_start(rows, kvs[s][0:count, :]).then_inc(kv_stored[s], 16)

                    with sp.Fori(0, PAIRS - 1) as i:
                        for s in range(2):
                            store(kv_table[bass.ds(i * (2 * R) + s * R, R), :], 2 * i + s, s)
                    store(kv_table[(T - 2) * R:(T - 1) * R, :], T - 2, 0)
                    store(kv_table[(T - 1) * R:N, :], T - 1, 1, RL)
                    for s in range(2):
                        sp.wait_ge(kv_stored[s], 16 * PAIRS)

        with ExitStack() as p2:
            J2 = [sb(f"J2_{s}", [128, G], I32, ctx=p2) for s in range(2)]
            MTf = [sb(f"MTf{s}", [R, E], ctx=p2) for s in range(2)]
            KV = [sb(f"KV{s}", [128, G, 2 * D], ctx=p2) for s in range(2)]
            V = [sb(f"V{s}", [128, G, D], ctx=p2) for s in range(2)]
            row2 = sb("row2", [128, G], I32, ctx=p2)
            row2b = sb("row2b", [128, G], BF16, ctx=p2)
            slot2 = sb("slot2", [128, G], I32, ctx=p2)
            M1 = [sb(f"M1_{s}", [128, G, 128], ctx=p2) for s in range(2)]
            slot_hot = [sb(f"slot_hot{s}", [128, G, SLOTS], ctx=p2) for s in range(2)]
            prod = sb("prod", [128, G, D], ctx=p2)
            sc = [sb(f"sc{s}", [128, G, H], ctx=p2) for s in range(2)]
            by_slot = sb("by_slot", [128, G * SLOTS * H + WIDE], ctx=p2)
            by_slot_edges = by_slot[:, 0:G * SLOTS * H].rearrange("p (g k h) -> p g k h", g=G, k=SLOTS)
            past = sb("past", [R, SLOTS], ctx=p2)
            masked = sb("masked", [R, SLOTS, H], ctx=p2)
            top = sb("top", [R, WIDE], ctx=p2)
            below = sb("below", [128, G, H], ctx=p2)
            PV = sb("PV", [128, G, D + H], ctx=p2)
            gate = Gate(sb, p2, "lists")

            rows_ready = sem("rows_ready", p2)
            v_kept = sem("v_kept", p2)
            MTf_ready = sem("MTf_ready", p2)
            kv_in = [sem(f"kv_in{s}", p2) for s in range(2)]
            q_spread = sem("q_spread", p2)
            prod_done = sem("prod_done", p2)
            by_slot_ready = sem("by_slot_ready", p2)
            slotted = sem("slotted", p2)
            top_ready = sem("top_ready", p2)
            top_spread = sem("top_spread", p2)
            below_ready = sem("below_ready", p2)
            p_ready = sem("p_ready", p2)
            pv_ready = sem("pv_ready", p2)
            att_ready = sem("att_ready", p2)
            att_read = sem("att_read", p2)
            z_ready = sem("z_ready", p2)
            ez_ready = sem("ez_ready", p2)
            order2 = sem("order2", p2)
            passed2 = sem("passed2", p2)

            ps_q, ps_slot, ps_top = ps[0:3], ps[3][0:R, 0:WIDE], ps[4][:, 0:(G - 1) * H + WIDE]
            ps_att = ps[5][0:R, 0:D + H]

            with nc.Block() as block:
                @block.gpsimd
                def _(pool):
                    def gather(t, s, first):
                        pool.wait_ge(rows_ready, t + 1)
                        if not first:
                            pool.wait_ge(prod_done, 3 * t - 3)
                            pool.wait_ge(v_kept, t - 1)
                        pool.sem_inc(passed2)
                        for g in range(G):
                            pool.indirect_dma_start(
                                out=KV[s][:, g, :], out_offset=None, in_=kv_table,
                                in_offset=bass.IndirectOffsetOnAxis(ap=J2[s][:, g:g + 1], axis=0),
                            ).then_inc(kv_in[s], 16)

                    for s in range(2):
                        gather(s, s, True)
                    with pool.Fori(1, PAIRS) as i:
                        for s in range(2):
                            gather(2 * i + s, s, False)

                @block.scalar
                def _(act):
                    a = nc.scalar

                    def rows(t, s, i, first):
                        if not first:
                            act.wait_ge(kv_in[s], 16 * G * i)
                        a.copy(J2[s][:], J_all[:, t, :]).then_inc(rows_ready, 1)

                    def hot_rows(t, s, first):
                        if not first:
                            act.wait_ge(top_spread, t - 1)
                        a.copy(MTf[s][:], MT_all[:, t, :]).then_inc(MTf_ready, 1)

                    def keep_v(t, s, i, first):
                        act.wait_ge(kv_in[s], 16 * G * i + 16 * G)
                        if not first:
                            act.wait_ge(pv_ready, t - 1)
                        a.copy(V[s][:], KV[s][:, :, D:2 * D]).then_inc(v_kept, 1)

                    def exps(t, first):
                        act.wait_ge(below_ready, t + 1)
                        if not first:
                            act.wait_ge(att_ready, t)
                        a.activation(PV[:, :, D:D + H], below[:], ACT.Exp, scale=SCALE).then_inc(p_ready, 1)

                    def gates(t):
                        act.wait_ge(z_ready, t + 1)
                        a.activation(gate.ez[:], gate.z2[:], ACT.Exp, scale=-1.0).then_inc(ez_ready, 1)

                    def step(t, s, i, prev=True, more3=True, more2=True, more1=True, first=False):
                        if more1:
                            keep_v(t + 1, 1 - s, i + s, first)
                        if more3:
                            rows(t + 3, 1 - s, i + 1 + s, False)
                        if more2:
                            hot_rows(t + 2, s, False)
                        if prev:
                            gates(t - 1)
                        exps(t, first)

                    for s in range(2):
                        rows(s, s, 0, True)
                        hot_rows(s, s, True)
                    keep_v(0, 0, 0, True)
                    rows(2, 0, 1, False)
                    step(0, 0, 0, prev=False, first=True)
                    step(1, 1, 0)
                    with act.Fori(1, PAIRS - 2) as i:
                        for s in range(2):
                            step(2 * i + s, s, i)
                    step(T - 4, 0, PAIRS - 2)
                    step(T - 3, 1, PAIRS - 2, more3=False)
                    step(T - 2, 0, PAIRS - 1, more3=False, more2=False)
                    step(T - 1, 1, PAIRS - 1, more3=False, more2=False, more1=False)
                    gates(T - 1)

                @block.tensor
                def _(pe):
                    mm = nc.tensor.matmul

                    def spread_q(t, s, first):
                        pe.wait_ge(MTf_ready, t + 1)
                        for c, (a, b) in enumerate(CHUNKS):
                            if not first:
                                pe.wait_ge(prod_done, 3 * t - 2 + c)
                            for g in range(a, b):
                                m = mm(ps_q[c][:, (g - a) * D:(g - a + 1) * D], MTf[s][:, g * 128:(g + 1) * 128],
                                       qx_all[:, t, 0, :], start=True, stop=True)
                            m.then_inc(q_spread, 1)

                    def spread_slot(t, s):
                        pe.wait_ge(by_slot_ready, t + 1)
                        for g in range(G):
                            m = mm(ps_slot, M1[s][:, g, 0:R], by_slot[:, g * SLOTS * H:g * SLOTS * H + WIDE],
                                   start=(g == 0), stop=(g == G - 1))
                        m.then_inc(slotted, 1)

                    def spread_top(t, s):
                        pe.wait_ge(top_ready, t + 1)
                        for g in range(G):
                            m = mm(ps_top[:, g * H:g * H + WIDE], MTf[s][:, g * 128:(g + 1) * 128], top[:],
                                   start=True, stop=True)
                        m.then_inc(top_spread, 1)

                    def attend(t, s, first):
                        pe.wait_ge(pv_ready, t + 1)
                        if not first:
                            pe.wait_ge(att_read, t)
                        for g in range(G):
                            m = mm(ps_att, M1[s][:, g, 0:R], PV[:, g, :], start=(g == 0), stop=(g == G - 1))
                        m.then_inc(att_ready, 1)

                    def step(t, s, first=False, more2=True, more1=True):
                        spread_top(t, s)
                        if more2:
                            spread_q(t + 2, s, False)
                        if more1:
                            spread_slot(t + 1, 1 - s)
                        attend(t, s, first)

                    spread_q(0, 0, True)
                    spread_slot(0, 0)
                    spread_q(1, 1, False)
                    step(0, 0, first=True)
                    step(1, 1)
                    with pe.Fori(1, PAIRS - 1) as i:
                        for s in range(2):
                            step(2 * i + s, s)
                    step(T - 2, 0, more2=False)
                    step(T - 1, 1, more2=False, more1=False)

                @block.vector
                def _(dve):
                    v = nc.vector
                    order = Count(dve, order2)

                    def scores(t, s, i):
                        for c, (a, b) in enumerate(CHUNKS):
                            dve.wait_ge(q_spread, 3 * t + c + 1)
                            if c == 0:
                                dve.wait_ge(kv_in[s], 16 * G * i + 16 * G)
                            v.tensor_tensor(prod[:, a:b, :], KV[s][:, a:b, 0:D],
                                            ps_q[c][:, 0:(b - a) * D].rearrange("p (g d) -> p g d", d=D),
                                            ALU.mult).then_inc(prod_done, 1)
                        dve.wait_ge(prod_done, 3 * t + 3)
                        return order.did(v.tensor_reduce(sc[s][:].rearrange("p g h -> p (g h)"),
                                                         prod[:].rearrange("p g (h c) -> p (g h) c", c=HC),
                                                         AX.X, ALU.add))

                    def spread_slots(t, s, scored):
                        order.at(scored)
                        v.tensor_tensor(by_slot_edges, slot_hot[s][:].unsqueeze(3).to_broadcast([128, G, SLOTS, H]),
                                        sc[s][:].unsqueeze(2).to_broadcast([128, G, SLOTS, H]),
                                        ALU.mult).then_inc(by_slot_ready, 1)

                    def slots_of(t, s):
                        order.did(v.tensor_scalar(row2[:], RS_all[:, t, :], 127, None, ALU.bitwise_and))
                        m = order.did(v.tensor_scalar(slot2[:], RS_all[:, t, :], 7, None, ALU.logical_shift_right))
                        order.at(m - 1)
                        m2 = order.did(v.tensor_copy(row2b[:], row2[:]))
                        order.at(m)
                        order.did(v.tensor_tensor(slot_hot[s][:], slot_of[:].unsqueeze(1).to_broadcast([128, G, SLOTS]),
                                                  slot2[:].unsqueeze(2).to_broadcast([128, G, SLOTS]), ALU.is_equal))
                        return m2

                    def hots(t, s, rows_known, first):
                        if not first:
                            dve.wait_ge(att_ready, t - 1)
                        order.at(rows_known)
                        order.did(v.tensor_tensor(M1[s][:], row_number[:].unsqueeze(1).to_broadcast([128, G, 128]),
                                                  row2b[:].unsqueeze(2).to_broadcast([128, G, 128]), ALU.is_equal))

                    def maximum(t, s):
                        m = order.did(v.tensor_tensor(past[:], slot_f[:], deg_all[:, bass.ds(t, 1)].to_broadcast([R, SLOTS]),
                                                      ALU.is_ge))
                        order.at(m)
                        dve.wait_ge(slotted, t + 1)
                        m = order.did(v.scalar_tensor_tensor(out=masked[:], in0=past[:].unsqueeze(2).to_broadcast([R, SLOTS, H]),
                                                             scalar=NEG, in1=ps_slot[:, 0:SLOTS * H].rearrange("p (k h) -> p k h", h=H),
                                                             op0=ALU.mult, op1=ALU.add))
                        order.at(m)
                        v.tensor_reduce(top[:, 0:H], masked[:].rearrange("p k h -> p h k"), AX.X, ALU.max).then_inc(top_ready, 1)

                    def subtract(t, s):
                        dve.wait_ge(top_spread, t + 1)
                        v.tensor_tensor(below[:].rearrange("p g h -> p (g h)"), sc[s][:].rearrange("p g h -> p (g h)"),
                                        ps_top[:, 0:G * H], ALU.subtract).then_inc(below_ready, 1)

                    def weigh(t, s):
                        dve.wait_ge(p_ready, t + 1)
                        v.tensor_tensor(PV[:, :, 0:D].rearrange("p g (h c) -> p g h c", c=HC),
                                        V[s][:].rearrange("p g (h c) -> p g h c", c=HC),
                                        PV[:, :, D:D + H].unsqueeze(3).to_broadcast([128, G, H, HC]),
                                        ALU.mult).then_inc(pv_ready, 1)

                    def step(t, s, i, now=True, more=True, prev=True, prev2=True, first_more=False):
                        if more:
                            known = slots_of(t + 1, 1 - s)
                        if now:
                            maximum(t, s)
                        if prev2:
                            dve.wait_ge(ez_ready, t - 1)
                            mix(v, order, x_all[:, t - 2, :], gl_all[:, t - 2, :], gate)
                        if prev:
                            dve.wait_ge(att_ready, t)
                            outcome(v, order, ps_att[:, 0:D], ps_att[:, D:D + H], att_read, t, wg,
                                    zx_all[:, bass.ds(t - 1, 1)], qx_all[:, t - 1, 1, :], gate, z_ready)
                        if more:
                            hots(t + 1, 1 - s, known, first_more)
                            scored = scores(t + 1, 1 - s, i + s)
                        if now:
                            subtract(t, s)
                        if more:
                            spread_slots(t + 1, 1 - s, scored)
                        if now:
                            weigh(t, s)

                    order.did(v.memset(top[:], 0.0))
                    order.did(v.memset(by_slot[:, G * SLOTS * H:], 0.0))
                    hots(0, 0, slots_of(0, 0), True)
                    scored = scores(0, 0, 0)
                    order.last()
                    spread_slots(0, 0, scored)
                    step(0, 0, 0, prev=False, prev2=False, first_more=True)
                    step(1, 1, 0, prev2=False)
                    start = order.n
                    with dve.Fori(1, PAIRS - 1) as i:
                        per_pair = 32
                        order.base = dve.snap(i * per_pair + (start - per_pair))
                        order.n = 0
                        for s in range(2):
                            step(2 * i + s, s, i)
                        assert order.n == per_pair, order.n
                    order.base, order.n = 0, start + (PAIRS - 2) * per_pair
                    step(T - 2, 0, PAIRS - 1)
                    step(T - 1, 1, PAIRS - 1, more=False)
                    step(T, 0, PAIRS, now=False, more=False)
                    step(T + 1, 1, PAIRS, now=False, more=False, prev=False)
                    order.last()

        with nc.If(nc.values_load(flag[0:1, 0:1], min_val=0, max_val=1)):
            dense_layer1(nc, sb, sem, ps, adj, kv_table, qx_all, zx_all, wg, x_all, ident, gl_all)

        with ExitStack() as p3:
            sq = sb("sq3", [R, T, D], ctx=p3)
            stats = [sb(f"stats3_{n}", [R, T], ctx=p3) for n in range(3)]
            order3 = sem("order3", p3)
            centred = sem("centred3", p3)
            squared = sem("squared3", p3)
            var_ready = sem("var_ready3", p3)
            std_ready = sem("std_ready3", p3)
            out_ready = sem("out_ready", p3)
            stored = sem("stored", p3)
            with nc.Block() as block:
                @block.vector
                def _(dve):
                    v = nc.vector
                    order = Count(dve, order3)
                    for n, (a, b) in enumerate(HALVES):
                        normed(v, order, gl_all, stats, a, b, centred, squared, std_ready, n, sq)
                    for n, (a, b) in enumerate(HALVES):
                        deviation(v, dve, order, stats, a, b, squared, var_ready, n + 1, sq)
                    for n, (a, b) in enumerate(HALVES):
                        inverse(v, dve, order, stats, a, b, std_ready, n + 1)
                        v.tensor_tensor(gl_all[:, a:b, :], gl_all[:, a:b, :],
                                        stats[2][:, a:b].unsqueeze(2).to_broadcast([R, b - a, D]),
                                        ALU.mult).then_inc(out_ready, 1)

                @block.scalar
                def _(act):
                    scalar_norm(nc.scalar, act, gl_all, stats, centred, squared, var_ready, std_ready, sq, 0)

                @block.sync
                def _(sp):
                    rows = out[0:(T - 1) * R, :].rearrange("(t p) d -> p t d", p=R)
                    sp.wait_ge(out_ready, 1)
                    a, b = HALVES[0]
                    sp.dma_start(rows[:, a:b, :], gl_all[:, a:b, :]).then_inc(stored, 16)
                    sp.wait_ge(out_ready, 2)
                    a, b = HALVES[1]
                    sp.dma_start(rows[:, a:b - 1, :], gl_all[:, a:b - 1, :]).then_inc(stored, 16)
                    sp.dma_start(out[(T - 1) * R:N, :], gl_all[0:RL, T - 1, :]).then_inc(stored, 16)
                    sp.wait_ge(stored, 48)


_INS = ['x', 'adj', 'L0_gnn_msg_w', 'L0_gnn_msg_b', 'L0_gnn_upd_w', 'L0_gnn_upd_b', 'L0_gnn_ln_w', 'L0_gnn_ln_b',
        'L1_gnn_Wq', 'L1_gnn_bq', 'L1_gnn_Wk', 'L1_gnn_bk', 'L1_gnn_Wv', 'L1_gnn_bv', 'L1_gnn_Ws', 'L1_gnn_bs',
        'L1_gnn_Wb']


def kernel(**inputs):
    import numpy as _np
    import concourse.bacc as _bacc
    from concourse import mybir as _mybir
    from concourse.bass_utils import run_bass_kernel_spmd as _run

    nc = _bacc.Bacc("TRN2", target_bir_lowering=False, num_devices=1)
    arrays, args = {}, []
    for name in _INS:
        a = _np.ascontiguousarray(inputs[name])
        arrays[f"in_{name}_dram"] = a
        args.append(nc.dram_tensor(f"in_{name}_dram", a.shape, _mybir.dt.from_np(a.dtype), kind="ExternalInput").ap())
    args.append(nc.dram_tensor("out_0_dram", (N, D), _mybir.dt.from_np(_np.dtype("float32")),
                               kind="ExternalOutput").ap())
    adj_resnorm_kernel(nc, *args)
    r = _run(nc, [arrays], core_ids=[0])
    return r.results[0]["out_0_dram"]
```

```python
import concourse.bass as bass
from concourse import mybir
from contextlib import ExitStack

ALU = mybir.AluOpType
ACT = mybir.ActivationFunctionType
F32 = mybir.dt.float32
BF16 = mybir.dt.bfloat16
I32 = mybir.dt.int32
U32 = mybir.dt.uint32
AX = mybir.AxisListType

N = 2708
D = 128
H, HC = 4, 32
R = 124
T = -(-N // R)
RL = N - (T - 1) * R
PAIRS = T // 2
BW = 2 * R
NB = -(-N // BW)
CAND = 8 * NB
SLOTS = 24
G = 10
E = G * 128
WIDE = 128
PAY = 3
GAP = 256 - BW
EPS = 1e-5
SCALE = float(HC) ** -0.5
NEG = -1.0e30
assert T % 2 == 0 and R < 128 and BW <= 256 and NB + 1 <= 15


class Count:

    def __init__(self, eng, sem, passed=None):
        self.eng, self.sem, self.passed, self.n, self.base = eng, sem, passed, 0, 0

    def did(self, instruction):
        instruction.then_inc(self.sem, 1)
        self.n += 1
        return self.n

    def at(self, mark):
        self.eng.wait_ge(self.sem, self.base + mark)

    def last(self):
        self.at(self.n)

    def at_apart(self, mark):
        self.at(mark)
        self.eng.sem_inc(self.passed)


def outcome(v, order, numerators, denominators, att_read, reads, wg, zx, skip, b, z_ready):
    m = order.did(v.tensor_scalar(b.den[:], denominators, 0.5, None, ALU.max))
    order.at(m)
    m = order.did(v.reciprocal(b.rden[:], b.den[:]))
    order.at(m)
    v.tensor_tensor(b.att[:].rearrange("p (c h) -> p h c", h=H), numerators.rearrange("p (h c) -> p h c", c=HC),
                    b.rden[:].unsqueeze(2).to_broadcast([R, H, HC]), ALU.mult).then_inc(att_read, 1)
    order.eng.wait_ge(att_read, reads)
    m = order.did(v.tensor_tensor_reduce(out=b.tmp[:], in0=b.att[:], in1=wg[:, 0, :], scale=1.0, scalar=0.0,
                                         op0=ALU.mult, op1=ALU.add, accum_out=b.z1[:]))
    order.at(m)
    v.tensor_tensor(b.z2[:], b.z1[:], zx, ALU.add).then_inc(z_ready, 1)
    order.did(v.tensor_tensor(b.diff[:], skip, b.att[:], ALU.subtract))


def mix(v, order, x1, result, b):
    m = order.did(v.tensor_scalar(b.ez[:], b.ez[:], 1.0, None, ALU.add))
    order.at(m)
    m = order.did(v.reciprocal(b.beta[:], b.ez[:]))
    order.at(m)
    m = order.did(v.scalar_tensor_tensor(out=b.tmp[:], in0=b.diff[:], scalar=b.beta[:, 0:1], in1=b.att[:],
                                         op0=ALU.mult, op1=ALU.add))
    order.at(m)
    return order.did(v.tensor_tensor(result, b.tmp[:], x1, ALU.add))


class Gate:

    def __init__(self, sb, ctx, name):
        def rows(part, width):
            return sb(f"{part}_{name}", [R, width], ctx=ctx)

        self.den, self.rden = rows("den", H), rows("rden", H)
        self.att, self.tmp, self.diff = rows("att", D), rows("tmp", D), rows("diff", D)
        self.z1, self.z2, self.ez, self.beta = rows("z1", 1), rows("z2", 1), rows("ez", 1), rows("beta", 1)


EARLY = 3
TILES_OF = [(n * (T - 3) // EARLY, (n + 1) * (T - 3) // EARLY) for n in range(EARLY)] + [(T - 3, T)]
NORM_CHUNKS = len(TILES_OF)


class Norm:

    def __init__(self, sb, sem, ctx, name, like=None):
        def rows(part):
            return sb(f"{part}_{name}", [R, T], ctx=ctx)

        if like is None:
            self.halves = sb(f"halves_{name}", [R, T, 6], ctx=ctx)
            self.mean2, self.gap, self.square, self.var = rows("mean2"), rows("gap"), rows("square"), rows("var")
            self.std, self.rstd, self.shift = rows("std"), rows("rstd"), rows("shift")
        else:
            self.halves, self.mean2, self.gap, self.square = like.halves, like.mean2, like.gap, like.square
            self.var, self.std, self.rstd, self.shift = like.var, like.std, like.rstd, like.shift
        self.h_ready = sem(f"h_ready_{name}", ctx)
        self.halves_ready = sem(f"halves_ready_{name}", ctx)
        self.var_ready = sem(f"var_ready_{name}", ctx)
        self.std_ready = sem(f"std_ready_{name}", ctx)
        self.shift_ready = sem(f"shift_ready_{name}", ctx)


def norm_variances(v, order, h, kept, n):
    lo, hi = TILES_OF[n]
    for t in range(lo, hi):
        v.bn_stats(kept.halves[:, t, :], h[:, t, :]).then_inc(kept.halves_ready, 1)
    order.eng.wait_ge(kept.halves_ready, hi)
    part = kept.halves[:, lo:hi, :]
    m = order.did(v.tensor_tensor(kept.gap[:, lo:hi], part[:, :, 1], part[:, :, 4], ALU.subtract))
    order.did(v.tensor_tensor(kept.mean2[:, lo:hi], part[:, :, 1], part[:, :, 4], ALU.add))
    order.did(v.tensor_tensor(kept.var[:, lo:hi], part[:, :, 2], part[:, :, 5], ALU.add))
    order.at(m)
    m = order.did(v.tensor_tensor(kept.square[:, lo:hi], kept.gap[:, lo:hi], kept.gap[:, lo:hi], ALU.mult))
    order.at(m)
    v.scalar_tensor_tensor(out=kept.var[:, lo:hi], in0=kept.square[:, lo:hi], scalar=D / 4.0,
                           in1=kept.var[:, lo:hi], op0=ALU.mult, op1=ALU.add).then_inc(kept.var_ready, 1)


def residual(v, order, h, x, kept, n):
    lo, hi = TILES_OF[n]
    v.tensor_tensor(h[:, lo:hi, :], h[:, lo:hi, :], x[:, lo:hi, :], ALU.add).then_inc(kept.h_ready, 1)
    order.eng.wait_ge(kept.h_ready, n + 1)
    norm_variances(v, order, h, kept, n)


def norm_deviations(a, act, kept, eps, n):
    lo, hi = TILES_OF[n]
    act.wait_ge(kept.var_ready, n + 1)
    a.activation(kept.std[:, lo:hi], kept.var[:, lo:hi], ACT.Sqrt, scale=1.0 / D, bias=eps[:, 0:1]).then_inc(
        kept.std_ready, 1)


def norm_shifts(v, order, kept, n):
    lo, hi = TILES_OF[n]
    order.eng.wait_ge(kept.std_ready, n + 1)
    m = order.did(v.reciprocal(kept.rstd[:, lo:hi], kept.std[:, lo:hi]))
    order.at(m)
    v.scalar_tensor_tensor(out=kept.shift[:, lo:hi], in0=kept.mean2[:, lo:hi], scalar=-0.5, in1=kept.rstd[:, lo:hi],
                           op0=ALU.mult, op1=ALU.mult).then_inc(kept.shift_ready, 1)


def norm_rows(a, act, h, kept, n, normed):
    act.wait_ge(kept.shift_ready, n + 1)
    for t in range(*TILES_OF[n]):
        a.activation(h[:, t, :], h[:, t, :], ACT.Identity, scale=kept.rstd[:, t:t + 1],
                     bias=kept.shift[:, t:t + 1]).then_inc(normed, 1)


def dense_layer0(nc, sb, sem, ps, adj, adj_row, d_table, s_all, u_all, updT, ident, gl_all, x_all, norm0):
    with ExitStack() as c:
        dT = sb("dense_dT", [D, T * R], ctx=c)
        sT = sb("dense_sT", [D, T * R], ctx=c)
        aggT = sb("dense_aggT", [D, T * R], ctx=c)
        d_in = sb("dense_d_in", [R, D], ctx=c)
        s_in = sb("dense_s_in", [R, D], ctx=c)
        msg = [sb(f"dense_msg{s}", [D, N], ctx=c) for s in range(2)]
        agg = [sb(f"dense_agg{s}", [D, 1], ctx=c) for s in range(2)]
        agg_tile = sb("dense_agg_tile", [D, R], ctx=c)
        cleared = sem("dense_cleared", c)
        d_loaded = sem("dense_d_loaded", c)
        s_copied = sem("dense_s_copied", c)
        turned = sem("dense_turned", c)
        kept = sem("dense_kept", c)
        row_in = [sem(f"dense_row_in{s}", c) for s in range(2)]
        msg_made = sem("dense_msg_made", c)
        agg_made = sem("dense_agg_made", c)
        agg_kept = sem("dense_agg_kept", c)
        tile_copied = sem("dense_tile_copied", c)
        summed = sem("dense_summed", c)
        done = sem("dense_done", c)
        again = Norm(sb, sem, c, "again", like=norm0)
        again_order = sem("again_order", c)
        with nc.Block() as block:
            @block.gpsimd
            def _(pool):
                nc.gpsimd.memset(d_in[:], 0.0).then_inc(cleared, 1)
                nc.gpsimd.memset(aggT[:], 0.0).then_inc(cleared, 1)

            @block.sync
            def _(sp):
                sp.wait_ge(cleared, 2)
                sp.dma_start(d_in[:], d_table[0:R, :]).then_inc(d_loaded, 16)
                with sp.Fori(1, T - 1) as t:
                    sp.wait_ge(turned, t)
                    sp.dma_start(d_in[:], d_table[bass.ds(t * R, R), :]).then_inc(d_loaded, 16)
                sp.wait_ge(turned, T - 1)
                sp.dma_start(d_in[0:RL, :], d_table[(T - 1) * R:N, :]).then_inc(d_loaded, 16)
                for s in range(2):
                    sp.dma_start(adj_row[s][:], adj[s:s + 1, :].to_broadcast([D, N])).then_inc(row_in[s], 16)
                with sp.Fori(1, N // 2) as i:
                    for s in range(2):
                        sp.wait_ge(agg_made, 2 * i + s - 1)
                        sp.dma_start(adj_row[s][:], adj[bass.ds(2 * i + s, 1), :].to_broadcast([D, N])).then_inc(
                            row_in[s], 16)

            @block.tensor
            def _(pe):
                pe.wait_ge(d_loaded, 16)
                pe.wait_ge(s_copied, 1)
                nc.tensor.transpose(ps[0][:, 0:R], d_in[:], ident[0:R, 0:R])
                nc.tensor.transpose(ps[0][:, R:2 * R], s_in[:], ident[0:R, 0:R]).then_inc(turned, 1)
                with pe.Fori(1, T) as t:
                    pe.wait_ge(d_loaded, 16 * t + 16)
                    pe.wait_ge(s_copied, t + 1)
                    pe.wait_ge(kept, 2 * t)
                    nc.tensor.transpose(ps[0][:, 0:R], d_in[:], ident[0:R, 0:R])
                    nc.tensor.transpose(ps[0][:, R:2 * R], s_in[:], ident[0:R, 0:R]).then_inc(turned, 1)
                with pe.Fori(0, T) as t:
                    pe.wait_ge(tile_copied, t + 1)
                    nc.tensor.matmul(ps[1][0:R, 0:D], ident[0:R, 0:R], u_all[:, t, :], start=True, stop=False)
                    nc.tensor.matmul(ps[1][0:R, 0:D], agg_tile[:], updT[:], start=False, stop=True).then_inc(summed, 1)

            @block.scalar
            def _(act):
                with act.Fori(0, T) as t:
                    act.wait_ge(turned, t + 1)
                    nc.scalar.copy(dT[:, bass.ds(t * R, R)], ps[0][:, 0:R]).then_inc(kept, 1)
                    nc.scalar.copy(sT[:, bass.ds(t * R, R)], ps[0][:, R:2 * R]).then_inc(kept, 1)
                act.wait_ge(kept, 2 * T)

                def message(n, s):
                    nc.scalar.activation(msg[s][:], dT[:, 0:N], ACT.Gelu, bias=sT[:, bass.ds(n, 1)]).then_inc(
                        msg_made, 1)

                for s in range(2):
                    message(s, s)
                with act.Fori(1, N // 2) as i:
                    for s in range(2):
                        act.wait_ge(agg_made, 2 * i + s - 1)
                        message(2 * i + s, s)
                with act.Fori(0, T) as t:
                    act.wait_ge(summed, t + 1)
                    nc.scalar.activation(gl_all[:, t, :], ps[1][0:R, 0:D], ACT.Gelu).then_inc(done, 1)
                act.wait_ge(done, T)

            @block.vector
            def _(dve):
                v = nc.vector
                v.tensor_copy(s_in[:], s_all[:, 0, :]).then_inc(s_copied, 1)
                with dve.Fori(1, T) as t:
                    dve.wait_ge(turned, t)
                    v.tensor_copy(s_in[:], s_all[:, t, :]).then_inc(s_copied, 1)
                dve.wait_ge(cleared, 2)
                with dve.Fori(0, N // 2) as i:
                    for s in range(2):
                        dve.wait_ge(row_in[s], 16 * i + 16)
                        dve.wait_ge(msg_made, 2 * i + s + 1)
                        v.tensor_tensor_reduce(out=msg[s][:], in0=msg[s][:], in1=adj_row[s][:], scale=1.0,
                                               scalar=0.0, op0=ALU.mult, op1=ALU.add,
                                               accum_out=agg[s][:]).then_inc(agg_made, 1)
                        dve.wait_ge(agg_made, 2 * i + s + 1)
                        v.tensor_copy(aggT[:, bass.ds(2 * i + s, 1)], agg[s][:]).then_inc(agg_kept, 1)
                dve.wait_ge(agg_kept, N)
                v.tensor_copy(agg_tile[:], aggT[:, 0:R]).then_inc(tile_copied, 1)
                with dve.Fori(1, T) as t:
                    dve.wait_ge(done, t)
                    v.tensor_copy(agg_tile[:], aggT[:, bass.ds(t * R, R)]).then_inc(tile_copied, 1)
                order = Count(dve, again_order)
                for n in range(EARLY):
                    dve.wait_ge(done, TILES_OF[n][1])
                    residual(v, order, gl_all, x_all, again, n)


def dense_layer1(nc, sb, sem, ps, adj, kv_table, qx_all, q_parts, zx_all, wg, x_all, ident, gl_all):
    COLS = [(a, min(N, a + 512)) for a in range(0, N, 512)]
    with ExitStack() as c:
        kT = sb("dense_kT", [D, T * R], ctx=c)
        V = sb("dense_V", [R, T, D], ctx=c)
        k_in = sb("dense_k_in", [R, D], ctx=c)
        q_in = sb("dense_q_in", [R, D], ctx=c)
        qT = sb("dense_qT", [D, R], ctx=c)
        qh = sb("dense_qh", [D, R], ctx=c)
        of_head = sb("dense_of_head", [D, H], ctx=c)
        adj_t = sb("dense_adj_t", [R, N], ctx=c)
        past = sb("dense_past", [R, N], ctx=c)
        e = sb("dense_e", [R, T * R], ctx=c)
        top = sb("dense_top", [R, 1], ctx=c)
        below = sb("dense_below", [R, 1], ctx=c)
        total = sb("dense_total", [R, 1], ctx=c)
        e_in = sb("dense_e_in", [R, R], ctx=c)
        eT = sb("dense_eT", [R, R], ctx=c)
        num = sb("dense_num", [R, H, HC], ctx=c)
        dens = sb("dense_dens", [R, H], ctx=c)
        gate = Gate(sb, c, "dense")
        made = sem("dense1_made", c)
        k_loaded = sem("dense1_k_loaded", c)
        v_loaded = sem("dense1_v_loaded", c)
        k_turned = sem("dense1_k_turned", c)
        k_kept = sem("dense1_k_kept", c)
        adj_loaded = sem("dense1_adj_loaded", c)
        q_copied = sem("dense1_q_copied", c)
        q_turned = sem("dense1_q_turned", c)
        qT_kept = sem("dense1_qT_kept", c)
        head_ready = sem("dense1_head_ready", c)
        scored = sem("dense1_scored", c)
        scores_read = sem("dense1_scores_read", c)
        below_ready = sem("dense1_below_ready", c)
        exp_done = sem("dense1_exp_done", c)
        e_copied = sem("dense1_e_copied", c)
        e_turned = sem("dense1_e_turned", c)
        eT_kept = sem("dense1_eT_kept", c)
        attended = sem("dense1_attended", c)
        head_done = sem("dense1_head_done", c)
        att_read = sem("dense1_att_read", c)
        z_ready = sem("dense1_z_ready", c)
        ez_ready = sem("dense1_ez_ready", c)
        tile_done = sem("dense1_tile_done", c)
        order_sem = sem("dense1_order", c)
        with nc.Block() as block:
            @block.gpsimd
            def _(pool):
                g = nc.gpsimd
                order = Count(pool, made)
                order.did(g.memset(V[:, T - 1, :], 0.0))
                order.did(g.memset(k_in[:], 0.0))
                order.did(g.memset(e[:, N:T * R], 0.0))
                order.did(g.memset(adj_t[:], 0.0))
                order.did(g.memset(of_head[:], 1.0))
                order.last()
                order.did(g.affine_select(out=of_head[:], in_=of_head[:], compare_op=ALU.is_ge, fill=0.0, base=0,
                                          pattern=[[-HC, H]], channel_multiplier=1))
                order.last()
                order.did(g.affine_select(out=of_head[:], in_=of_head[:], compare_op=ALU.is_ge, fill=0.0,
                                          base=HC - 1, pattern=[[HC, H]], channel_multiplier=-1))

            @block.sync
            def _(sp):
                sp.wait_ge(made, 7)
                v_rows = kv_table[0:(T - 1) * R, D:2 * D].rearrange("(t p) d -> p t d", p=R)
                sp.dma_start(V[:, 0:T - 1, :], v_rows).then_inc(v_loaded, 16)
                sp.dma_start(V[0:RL, T - 1, :], kv_table[(T - 1) * R:N, D:2 * D]).then_inc(v_loaded, 16)
                sp.dma_start(k_in[:], kv_table[0:R, 0:D]).then_inc(k_loaded, 16)
                with sp.Fori(1, T - 1) as t:
                    sp.wait_ge(k_turned, t)
                    sp.dma_start(k_in[:], kv_table[bass.ds(t * R, R), 0:D]).then_inc(k_loaded, 16)
                sp.wait_ge(k_turned, T - 1)
                sp.dma_start(k_in[0:RL, :], kv_table[(T - 1) * R:N, 0:D]).then_inc(k_loaded, 16)
                sp.dma_start(adj_t[:], adj[0:R, :]).then_inc(adj_loaded, 16)
                with sp.Fori(1, T - 1) as t:
                    sp.wait_ge(tile_done, t)
                    sp.dma_start(adj_t[:], adj[bass.ds(t * R, R), :]).then_inc(adj_loaded, 16)
                sp.wait_ge(tile_done, T - 1)
                sp.dma_start(adj_t[0:RL, :], adj[(T - 1) * R:N, :]).then_inc(adj_loaded, 16)
                sp.wait_ge(v_loaded, 32)

            @block.tensor
            def _(pe):
                def turn_k(t):
                    pe.wait_ge(k_loaded, 16 * t + 16)
                    nc.tensor.transpose(ps[0][:, 0:R], k_in[:], ident[0:R, 0:R]).then_inc(k_turned, 1)

                turn_k(0)
                with pe.Fori(1, T) as t:
                    pe.wait_ge(k_kept, t)
                    turn_k(t)
                pe.wait_ge(k_kept, T)
                pe.wait_ge(v_loaded, 32)
                with pe.Fori(0, T) as t:
                    pe.wait_ge(q_copied, t + 1)
                    nc.tensor.transpose(ps[6][:, 0:R], q_in[:], ident[0:R, 0:R]).then_inc(q_turned, 1)
                    with pe.Fori(0, H) as h:
                        pe.wait_ge(head_ready, t * H + h + 1)
                        for n, (a, b) in enumerate(COLS):
                            m = nc.tensor.matmul(ps[n][0:R, 0:b - a], qh[:], kT[:, a:b], start=True, stop=True)
                        m.then_inc(scored, 1)

                        def weigh(j, start):
                            pe.wait_ge(e_copied, (t * H + h) * T + j + 1)
                            nc.tensor.transpose(ps[6][0:R, 0:R], e_in[:], ident[0:R, 0:R]).then_inc(e_turned, 1)
                            pe.wait_ge(eT_kept, (t * H + h) * T + j + 1)
                            nc.tensor.matmul(ps[7][0:R, 0:HC], eT[:], V[:, j, :][:, bass.ds(h * HC, HC)],
                                             start=start, stop=True, skip_group_check=True).then_inc(attended, 1)

                        weigh(0, True)
                        with pe.Fori(1, T) as j:
                            weigh(j, False)

            @block.scalar
            def _(act):
                a_ = nc.scalar
                with act.Fori(0, T) as t:
                    act.wait_ge(k_turned, t + 1)
                    a_.copy(kT[:, bass.ds(t * R, R)], ps[0][:, 0:R]).then_inc(k_kept, 1)
                with act.Fori(0, T) as t:
                    act.wait_ge(q_turned, t + 1)
                    a_.copy(qT[:], ps[6][:, 0:R]).then_inc(qT_kept, 1)
                    with act.Fori(0, H) as h:
                        act.wait_ge(below_ready, t * H + h + 1)
                        a_.activation(e[:, 0:N], e[:, 0:N], ACT.Exp, bias=below[:, 0:1]).then_inc(exp_done, 1)
                        with act.Fori(0, T) as j:
                            act.wait_ge(e_turned, (t * H + h) * T + j + 1)
                            a_.copy(eT[:], ps[6][0:R, 0:R]).then_inc(eT_kept, 1)
                    act.wait_ge(z_ready, t + 1)
                    a_.activation(gate.ez[:], gate.z2[:], ACT.Exp, scale=-1.0).then_inc(ez_ready, 1)

            @block.vector
            def _(dve):
                v = nc.vector
                dve.wait_ge(made, 7)
                order = Count(dve, order_sem)
                PER_HEAD, PER_TILE = 3, 9
                with dve.Fori(0, T) as t:
                    order.base, order.n = dve.snap(t * (PER_TILE + H * PER_HEAD)), 0
                    v.tensor_tensor(q_in[:], qx_all[:, t, 0, :], q_parts[:, t, 0, :], ALU.add).then_inc(q_copied, 1)
                    dve.wait_ge(adj_loaded, 16 * t + 16)
                    m = order.did(v.tensor_scalar(past[:], adj_t[:], 0.0, NEG, ALU.is_equal, ALU.mult))
                    with dve.Fori(0, H) as h:
                        done = t * H + h + 1
                        dve.wait_ge(qT_kept, t + 1)
                        v.tensor_tensor(qh[:], qT[:], of_head[:, bass.ds(h, 1)].to_broadcast([D, R]),
                                        ALU.mult).then_inc(head_ready, 1)
                        order.at(m)
                        dve.wait_ge(scored, done)
                        for n, (a, b) in enumerate(COLS):
                            v.scalar_tensor_tensor(out=e[:, a:b], in0=ps[n][0:R, 0:b - a], scalar=SCALE,
                                                   in1=past[:, a:b], op0=ALU.mult, op1=ALU.add).then_inc(scores_read, 1)
                        in_head = t * (PER_TILE + H * PER_HEAD) + h * PER_HEAD
                        dve.wait_ge(scores_read, done * len(COLS))
                        v.tensor_reduce(top[:], e[:, 0:N], AX.X, ALU.max).then_inc(order_sem, 1)
                        dve.wait_ge(order_sem, in_head + 2)
                        v.tensor_scalar(below[:], top[:], -1.0, None, ALU.mult).then_inc(below_ready, 1)
                        dve.wait_ge(exp_done, done)
                        v.scalar_tensor_tensor(out=e[:, 0:N], in0=adj_t[:], scalar=0.0, in1=e[:, 0:N],
                                               op0=ALU.not_equal, op1=ALU.mult, accum_out=total[:]).then_inc(order_sem, 1)
                        dve.wait_ge(order_sem, in_head + 3)
                        v.tensor_copy(dens[:, bass.ds(h, 1)], total[:]).then_inc(order_sem, 1)
                        v.tensor_copy(e_in[:], e[:, 0:R]).then_inc(e_copied, 1)
                        with dve.Fori(1, T) as j:
                            dve.wait_ge(attended, (done - 1) * T + j)
                            v.tensor_copy(e_in[:], e[:, bass.ds(j * R, R)]).then_inc(e_copied, 1)
                        dve.wait_ge(attended, done * T)
                        v.tensor_copy(num[:, bass.ds(h, 1), :].rearrange("p a c -> p (a c)"),
                                      ps[7][0:R, 0:HC]).then_inc(head_done, 1)
                    order.n += H * PER_HEAD
                    dve.wait_ge(head_done, t * H + H)
                    order.last()
                    outcome(v, order, num[:].rearrange("p h c -> p (h c)"), dens[:], att_read, t + 1, wg,
                            zx_all[:, bass.ds(t, 1)], qx_all[:, t, 1, :], gate, z_ready)
                    dve.wait_ge(ez_ready, t + 1)
                    order.last()
                    m = mix(v, order, x_all[:, t, :], gl_all[:, t, :], gate)
                    order.at(m)
                    assert order.n == PER_TILE + H * PER_HEAD, order.n
                    dve.sem_inc(tile_done)


def adj_resnorm_kernel(nc, x, adj, msg_w, msg_b, upd_w, upd_b, ln_w, ln_b,
                       Wq, bq, Wk, bk, Wv, bv, Ws, bs, Wb, out, debug=None):
    with ExitStack() as whole:
        def sb(name, shape, dt=F32, ctx=whole):
            return ctx.enter_context(nc.sbuf_tensor(name, shape, dt))

        def sem(name, ctx=whole):
            return ctx.enter_context(nc.semaphore(name))

        d_table = nc.dram_tensor("d_table", (N, D), F32, kind="Internal").ap()
        kv_table = nc.dram_tensor("kv_table", (N, 2 * D), F32, kind="Internal").ap()

        ident = sb("ident", [128, 128])
        ident_bf = sb("ident_bf", [128, 128], BF16)
        before = sb("before", [R, R])
        block_code = sb("block_code", [R, NB, 8], I32)
        slot_f = sb("slot_f", [R, SLOTS])
        rowslot = sb("rowslot", [R, SLOTS])
        group_i = sb("group_i", [R, G], I32)
        lane_i = sb("lane_i", [R, 128 + SLOTS], I32)
        row_number = sb("row_number", [128, 128], BF16)
        slot_of = sb("slot_of", [128, SLOTS], I32)

        x_all = sb("x_all", [R, T, D])
        MT_all = sb("MT_all", [R, T, E], BF16)
        J_all = sb("J_all", [128, T, G], I32)
        RS_all = sb("RS_all", [128, T, G], I32)
        deg_all = sb("deg_all", [R, T])
        bad = sb("bad", [R, 1])
        gl_all = sb("gl_all", [R, T, D])
        w1 = sb("w1", [D, 4, D])
        b1 = sb("b1", [R, 4, D])
        wb = sb("wb", [R, 3, D])
        ln = sb("ln", [R, 2, D])
        eps = sb("eps", [R, 1])
        norm0 = Norm(sb, sem, whole, "inner")
        flag = sb("flag", [1, 1], I32)
        late_in = sem("late_in")

        ps = [whole.enter_context(nc.psum_tensor(f"ps{n}", [128, 512], F32)) for n in range(8)]

        STORES = ((0, 8, 8), (8, 16, 16), (16, T - 1, T))

        mid = ExitStack()
        whole.enter_context(mid)
        s_all = sb("s_all", [R, T, D], ctx=mid)
        u_all = sb("u_all", [R, T, D], ctx=mid)
        updT = sb("updT", [D, D], ctx=mid)
        d_all = sb("d_all", [R, T, D], ctx=mid)
        d_stored = sem("d_stored", mid)
        adj_t = [sb(f"adj{s}", [D, N], ctx=mid) for s in range(2)]
        adj_loaded = [sem(f"adj_loaded{s}", mid) for s in range(2)]
        with ExitStack() as p0:
            w_in = sb("w_in", [D, 4, D], ctx=p0)
            wT = sb("wT", [D, 3, D], ctx=p0)
            bias0 = sb("bias0", [128, 3, D], ctx=p0)
            xin = [sb(f"xin{s}", [R, D], ctx=p0) for s in range(2)]
            xT = [sb(f"xT{s}", [D, R], ctx=p0) for s in range(2)]
            const_made = sem("const_made", p0)
            vconst = sem("vconst", p0)
            weights_in = sem("weights_in", p0)
            x_first = sem("x_first", p0)
            x_rest = sem("x_rest", p0)
            x_in = sem("x_in", p0)
            w_turned = sem("w_turned", p0)
            updT_ready = sem("updT_ready", p0)
            wT_ready = sem("wT_ready", p0)
            x_turned = sem("x_turned", p0)
            xT_ready = sem("xT_ready", p0)
            projected = sem("projected", p0)
            biased = sem("biased", p0)
            MADE, ZEROED = 14, 5
            with nc.Block() as block:
                @block.gpsimd
                def _(pool):
                    g = nc.gpsimd
                    order = Count(pool, const_made)
                    order.did(g.memset(ident[:], 0.0))
                    order.did(g.memset(before[:], 1.0))
                    order.did(g.memset(x_all[:, T - 1, :], 0.0))
                    order.did(g.memset(bad[:], 0.0))
                    order.did(g.memset(eps[:], EPS))
                    order.last()
                    order.did(g.affine_select(out=ident[:], in_=ident[:], compare_op=ALU.not_equal, fill=1.0,
                                              base=0, pattern=[[-1, 128]], channel_multiplier=1))
                    order.did(g.affine_select(out=before[:], in_=before[:], compare_op=ALU.is_gt, fill=0.0,
                                              base=0, pattern=[[1, R]], channel_multiplier=-1))
                    order.did(g.iota(block_code[:], pattern=[[1, NB], [0, 8]], base=1, channel_multiplier=0))
                    order.did(g.iota(slot_f[:], pattern=[[1, SLOTS]], base=0, channel_multiplier=0,
                                     allow_small_or_imprecise_dtypes=True))
                    order.did(g.iota(rowslot[:], pattern=[[128, SLOTS]], base=1, channel_multiplier=1,
                                     allow_small_or_imprecise_dtypes=True))
                    order.did(g.iota(group_i[:], pattern=[[1, G]], base=0, channel_multiplier=0))
                    order.did(g.iota(lane_i[:], pattern=[[1, 128 + SLOTS]], base=128 - SLOTS,
                                     channel_multiplier=0))
                    order.did(g.iota(row_number[:], pattern=[[1, 128]], base=1, channel_multiplier=0,
                                     allow_small_or_imprecise_dtypes=True))
                    order.did(g.iota(slot_of[:], pattern=[[1, SLOTS]], base=0, channel_multiplier=0))
                    made = order.n
                    assert made == MADE

                    def place(t, s):
                        g.tensor_copy(xin[s][:], x_all[:, t, :]).then_inc(x_in, 1)

                    pool.wait_ge(x_first, 16)
                    for s in range(2):
                        place(s, s)
                    pool.wait_ge(x_rest, 32)
                    with pool.Fori(1, PAIRS) as i:
                        for s in range(2):
                            pool.wait_ge(x_turned, 2 * i + s - 1)
                            place(2 * i + s, s)

                @block.sync
                def _(sp):
                    sp.dma_start(w_in[:, 0:2, :], msg_w.rearrange("o (h d) -> o h d", h=2)).then_inc(weights_in, 16)
                    sp.dma_start(w_in[:, 2:4, :], upd_w.rearrange("o (h d) -> o h d", h=2)).then_inc(weights_in, 16)
                    x_rows = x[0:(T - 1) * R, :].rearrange("(t p) d -> p t d", p=R)
                    sp.dma_start(x_all[:, 0:2, :], x_rows[:, 0:2, :]).then_inc(x_first, 16)
                    sp.dma_start(bias0[:, 1, :], msg_b[None, :].to_broadcast([128, D])).then_inc(weights_in, 16)
                    sp.dma_start(bias0[:, 2, :], upd_b[None, :].to_broadcast([128, D])).then_inc(weights_in, 16)
                    sp.dma_start(x_all[:, 2:T - 1, :], x_rows[:, 2:, :]).then_inc(x_rest, 16)
                    sp.wait_ge(const_made, ZEROED)
                    sp.dma_start(x_all[0:RL, T - 1, :], x[(T - 1) * R:N, :]).then_inc(x_rest, 16)
                    for s in range(2):
                        sp.dma_start(adj_t[s][0:R, :], adj[s * R:(s + 1) * R, :]).then_inc(adj_loaded[s], 16)
                    for n, w in enumerate((Wk, Wv, Wq, Ws)):
                        sp.dma_start(w1[:, n, :], w).then_inc(late_in, 16)
                    for n, b in enumerate((bk, bv, bq, bs)):
                        sp.dma_start(b1[:, n, :], b[None, :].to_broadcast([R, D])).then_inc(late_in, 16)
                    for n, b in enumerate((ln_w, ln_b)):
                        sp.dma_start(ln[:, n, :], b[None, :].to_broadcast([R, D])).then_inc(late_in, 16)
                    sp.dma_start(wb[:].rearrange("p a d -> p (a d)"),
                                 Wb.rearrange("d a -> a d").to_broadcast([R, 3 * D])).then_inc(late_in, 16)
                    d_rows = d_table[0:(T - 1) * R, :].rearrange("(t p) d -> p t d", p=R)
                    for a, b, after in STORES:
                        sp.wait_ge(biased, after)
                        sp.dma_start(d_rows[:, a:b, :], d_all[:, a:b, :]).then_inc(d_stored, 16)
                    sp.dma_start(d_table[(T - 1) * R:N, :], d_all[0:RL, T - 1, :]).then_inc(d_stored, 16)

                @block.tensor
                def _(pe):
                    pe.wait_ge(const_made, MADE)
                    pe.wait_ge(weights_in, 64)
                    for n, half in enumerate((1, 0, 2, 3)):
                        o = ps[4][:, n * D:(n + 1) * D] if n < 3 else ps[5][:, 0:D]
                        m = nc.tensor.transpose(o, w_in[:, half, :], ident[:])
                    m.then_inc(w_turned, 1)

                    def turn(t, s):
                        pe.wait_ge(x_in, t + 1)
                        nc.tensor.transpose(ps[s][:, 0:R], xin[s][:], ident[0:R, 0:R]).then_inc(x_turned, 1)

                    def project(t, s, first):
                        pe.wait_ge(xT_ready, t + 1)
                        if not first:
                            pe.wait_ge(biased, t - 1)
                        nc.tensor.matmul(ps[2 + s][0:R, 0:3 * D], xT[s][:], wT[:].rearrange("d h o -> d (h o)"),
                                         start=True, stop=True).then_inc(projected, 1)

                    pe.wait_ge(wT_ready, 1)
                    turn(0, 0)
                    turn(1, 1)
                    project(0, 0, True)
                    turn(2, 0)
                    project(1, 1, True)
                    with pe.Fori(1, PAIRS - 1) as i:
                        turn(2 * i + 1, 1)
                        project(2 * i, 0, False)
                        turn(2 * i + 2, 0)
                        project(2 * i + 1, 1, False)
                    turn(T - 1, 1)
                    project(T - 2, 0, False)
                    project(T - 1, 1, False)

                @block.scalar
                def _(act):
                    act.wait_ge(const_made, MADE)
                    nc.scalar.copy(ident_bf[:], ident[:]).then_inc(updT_ready, 1)
                    act.wait_ge(w_turned, 1)
                    nc.scalar.copy(updT[:], ps[5][:, 0:D]).then_inc(updT_ready, 1)

                    def take(s, t1):
                        act.wait_ge(x_turned, t1)
                        nc.scalar.copy(xT[s][:], ps[s][:, 0:R]).then_inc(xT_ready, 1)

                    for s in range(2):
                        take(s, s + 1)
                    with act.Fori(1, PAIRS) as i:
                        for s in range(2):
                            act.wait_ge(projected, 2 * i + s - 1)
                            take(s, 2 * i + s + 1)

                @block.vector
                def _(dve):
                    v = nc.vector
                    dve.wait_ge(const_made, MADE)
                    order = Count(dve, vconst)
                    order.did(v.memset(bias0[:, 0, :], 0.0))
                    order.did(v.tensor_scalar(block_code[:], block_code[:], 27, None, ALU.logical_shift_left))
                    order.did(v.tensor_scalar(lane_i[:], lane_i[:], 127, None, ALU.bitwise_and))
                    order.last()
                    dve.wait_ge(w_turned, 1)
                    v.tensor_copy(wT[:].rearrange("d h o -> d (h o)"), ps[4][:, 0:3 * D]).then_inc(wT_ready, 1)
                    dve.wait_ge(weights_in, 64)

                    def add_bias(t, s, after):
                        dve.wait_ge(projected, after)
                        v.tensor_copy(d_all[:, t, :], ps[2 + s][0:R, 0:D])
                        v.tensor_tensor(s_all[:, t, :], ps[2 + s][0:R, D:2 * D], bias0[0:R, 1, :], ALU.add)
                        v.tensor_tensor(u_all[:, t, :], ps[2 + s][0:R, 2 * D:3 * D], bias0[0:R, 2, :],
                                        ALU.add).then_inc(biased, 1)

                    with dve.Fori(0, PAIRS) as i:
                        for s in range(2):
                            add_bias(i * 2 + s, s, 2 * i + s + 1)
                    dve.wait_ge(biased, T)

        with ExitStack() as p1:
            sgn = sb("sgn", [R, N], BF16, ctx=p1)
            nz = [sb(f"nz{s}", [R, 1], ctx=p1) for s in range(2)]
            cw = sb("cw", [R, CAND], ctx=p1)
            ci = sb("ci", [R, CAND], U32, ctx=p1)
            code = sb("code", [R, CAND], I32, ctx=p1)
            keys = [sb(f"keys{n}", [R, CAND], ctx=p1) for n in range(2)]
            keys_b = [sb(f"keys_b{n}", [R, CAND], ctx=p1) for n in range(2)]
            best = [sb(f"best{n}", [R, SLOTS], ctx=p1) for n in range(2)]
            valid = sb("valid", [R, SLOTS], ctx=p1)
            deg = sb("deg", [R, WIDE], ctx=p1)
            jcode = sb("jcode", [R, SLOTS], I32, ctx=p1)
            blk = sb("blk", [R, SLOTS], I32, ctx=p1)
            node = sb("node", [128, G], ctx=p1)
            whigh = sb("whigh", [R, SLOTS], I32, ctx=p1)
            pay = sb("pay", [R, SLOTS, PAY], ctx=p1)
            off = sb("off", [R, 1], ctx=p1)
            end = sb("end", [R, 1], ctx=p1)
            pos = sb("pos", [R, SLOTS], I32, ctx=p1)
            grp = sb("grp", [R, SLOTS], I32, ctx=p1)
            lane = sb("lane", [R, 1], I32, ctx=p1)
            lane_hot = sb("lane_hot", [R, 128 + SLOTS], ctx=p1)
            grp_hot = sb("grp_hot", [R, SLOTS, G], ctx=p1)
            rhs = sb("rhs", [R, SLOTS * G * PAY + WIDE], ctx=p1)
            rhs_slots = rhs[:, 0:SLOTS * G * PAY].rearrange("p (k g a) -> p k g a", k=SLOTS, g=G)
            J = [sb(f"J{s}", [128, G], I32, ctx=p1) for s in range(2)]
            RS = [sb(f"RS{s}", [128, G], I32, ctx=p1) for s in range(2)]
            row_i = sb("row_i", [128, G], I32, ctx=p1)
            row_b = sb("row_b", [128, G], BF16, ctx=p1)
            w_e = [sb(f"w_e{s}", [128, G], ctx=p1) for s in range(2)]
            M = [sb(f"M{s}", [128, G, 128], BF16, ctx=p1) for s in range(2)]
            Mw = [sb(f"Mw{s}", [128, G, 128], ctx=p1) for s in range(2)]
            MT = [sb(f"MT{s}", [R, E], ctx=p1) for s in range(2)]
            gath = [sb(f"gath{s}", [128, G, D], ctx=p1) for s in range(2)]
            msg = sb("msg", [128, G, D], ctx=p1)
            aggT = sb("aggT", [D, R], ctx=p1)

            adj_scanned = sem("adj_scanned", p1)
            adj_counted = sem("adj_counted", p1)
            deg_ready = sem("deg_ready", p1)
            filled = sem("filled", p1)
            off_ready = sem("off_ready", p1)
            slots_ready = sem("slots_ready", p1)
            packed = sem("packed", p1)
            index_ready = sem("index_ready", p1)
            lists_kept = sem("lists_kept", p1)
            hot_ready = sem("hot_ready", p1)
            mw_ready = sem("mw_ready", p1)
            hot_turned = sem("hot_turned", p1)
            MT_ready = sem("MT_ready", p1)
            gathered = [sem(f"gathered{s}", p1) for s in range(2)]
            sums_ready = sem("sums_ready", p1)
            msg_ready = sem("msg_ready", p1)
            agg_ready = sem("agg_ready", p1)
            aggT_ready = sem("aggT_ready", p1)
            upd_ready = sem("upd_ready", p1)
            gl_ready = sem("gl_ready", p1)
            dve_order = sem("dve_order", p1)
            dve_passed = sem("dve_passed", p1)
            pool_passed = sem("pool_passed", p1)
            act_order = sem("act_order", p1)

            ps_msg = ps[0:3]
            ps_turn = [ps[n][:].bitcast(BF16) for n in (3, 4)]
            ps_off, ps_pack = ps[7][0:R, 0:WIDE], ps[5][:, 0:WIDE]
            ps_agg, ps_upd = ps[6][:, 0:R], ps[6][0:R, 128:128 + D]
            CHUNKS = [(0, 4), (4, 8), (8, G)]

            with nc.Block() as block:
                @block.sync
                def _(sp):
                    with sp.Fori(1, PAIRS - 1) as i:
                        for s in range(2):
                            sp.wait_ge(adj_scanned, 2 * i + s - 1)
                            sp.wait_ge(adj_counted, 2 * i + s - 1)
                            sp.dma_start(adj_t[s][0:R, :], adj[bass.ds(i * (2 * R) + s * R, R), :]).then_inc(
                                adj_loaded[s], 16)
                    sp.wait_ge(adj_scanned, T - 3)
                    sp.wait_ge(adj_counted, T - 3)
                    sp.dma_start(adj_t[0][0:R, :], adj[(T - 2) * R:(T - 1) * R, :]).then_inc(adj_loaded[0], 16)
                    sp.wait_ge(adj_scanned, T - 2)
                    sp.wait_ge(adj_counted, T - 2)
                    sp.dma_start(adj_t[1][0:RL, :], adj[(T - 1) * R:N, :]).then_inc(adj_loaded[1], 16)
                    sp.wait_ge(late_in, 16 * 11)

                @block.gpsimd
                def _(pool):
                    def gather(t, s, i, first):
                        pool.wait_ge(index_ready, t + 1)
                        if not first:
                            pool.wait_ge(sums_ready, 3 * t - 3)
                        pool.sem_inc(pool_passed)
                        for g in range(G):
                            pool.indirect_dma_start(
                                out=gath[s][:, g, :], out_offset=None, in_=d_table,
                                in_offset=bass.IndirectOffsetOnAxis(ap=J[s][:, g:g + 1], axis=0),
                            ).then_inc(gathered[s], 16)
                        pool.wait_ge(hot_ready, t + 1)
                        if not first:
                            pool.wait_ge(agg_ready, t - 1)
                        nc.gpsimd.tensor_tensor(Mw[s][:], M[s][:], w_e[s][:].unsqueeze(2).to_broadcast([128, G, 128]),
                                                ALU.mult).then_inc(mw_ready, 1)
                        nc.gpsimd.tensor_copy(J_all[:, t, :], J[s][:]).then_inc(lists_kept, 1)
                        nc.gpsimd.tensor_copy(RS_all[:, t, :], RS[s][:]).then_inc(lists_kept, 1)

                    nc.gpsimd.memset(deg[:], 0.0).then_inc(filled, 1)
                    nc.gpsimd.memset(rhs[:, SLOTS * G * PAY:], 0.0).then_inc(filled, 1)
                    pool.wait_ge(d_stored, 16 * (len(STORES) + 1))
                    for s in range(2):
                        gather(s, s, 0, True)
                    with pool.Fori(1, PAIRS) as i:
                        for s in range(2):
                            gather(2 * i + s, s, i, False)
                    pool.wait_ge(lists_kept, 2 * T)

                @block.vector
                def _(dve):
                    v = nc.vector
                    order = Count(dve, dve_order, dve_passed)

                    def scan_weights(t, s, i):
                        dve.wait_ge(adj_loaded[s], 16 * i + 16)
                        dve.sem_inc(dve_passed)
                        for b in range(NB):
                            order.did(v.max(out=cw[:, 8 * b:8 * b + 8], in_=adj_t[s][0:R, b * BW:min(N, (b + 1) * BW)]))

                    def scan_columns(t, s):
                        order.at_apart(order.n)
                        for b in range(NB):
                            m = v.max_index(out=ci[:, 8 * b:8 * b + 8], in_max=cw[:, 8 * b:8 * b + 8],
                                            in_values=adj_t[s][0:R, b * BW:min(N, (b + 1) * BW)])
                            if b < NB - 1:
                                order.did(m)
                        m.then_inc(adj_scanned, 1)

                    def slots(t, s):
                        bits = cw[:].bitcast(I32)
                        flat = block_code[:].rearrange("p b e -> p (b e)")
                        dve.wait_ge(adj_scanned, t + 1)
                        m = order.did(v.scalar_tensor_tensor(out=code[:], in0=ci[:].bitcast(I32), scalar=19, in1=flat,
                                                             op0=ALU.logical_shift_left, op1=ALU.bitwise_or))
                        order.at(m)
                        order.did(v.scalar_tensor_tensor(out=keys_b[0][:].bitcast(I32), in0=bits, scalar=12,
                                                         in1=code[:], op0=ALU.logical_shift_right,
                                                         op1=ALU.bitwise_or))
                        m = order.did(v.scalar_tensor_tensor(out=keys_b[1][:].bitcast(I32), in0=bits, scalar=0xFFF,
                                                             in1=code[:], op0=ALU.bitwise_and, op1=ALU.bitwise_or))
                        for n in range(2):
                            order.at(m - 1 + n)
                            m2 = order.did(v.scalar_tensor_tensor(out=keys[n][:], in0=cw[:], scalar=0.0,
                                                                  in1=keys_b[n][:], op0=ALU.is_gt, op1=ALU.mult))
                        for r in range(SLOTS // 8):
                            src = keys if r % 2 == 0 else keys_b
                            dst_ = keys_b if r % 2 == 0 else keys
                            for n in range(2):
                                order.at_apart(m2 - 1 + n)
                                m3 = order.did(v.max(out=best[n][:, 8 * r:8 * r + 8], in_=src[n][:]))
                            m2 = m3
                            if r < SLOTS // 8 - 1:
                                for n in range(2):
                                    order.at_apart(m3 - 1 + n)
                                    m2 = order.did(v.match_replace(out=dst_[n][:], in_to_replace=best[n][:, 8 * r:8 * r + 8],
                                                                   in_values=src[n][:], imm_value=0.0))
                        order.at(m2 - 1)
                        order.did(v.tensor_scalar(valid[:], best[0][:], 0.0, 0.0, ALU.is_gt, ALU.add,
                                                  accum_out=deg[:, 0:1]))
                        order.did(v.tensor_scalar(jcode[:], best[0][:].bitcast(I32), 19, None,
                                                  ALU.logical_shift_right))
                        order.did(v.tensor_scalar(blk[:], best[0][:].bitcast(I32), 27, None,
                                                  ALU.logical_shift_right))
                        m = order.did(v.tensor_scalar(whigh[:], best[0][:].bitcast(I32), 0x7FFFF, 12,
                                                      ALU.bitwise_and, ALU.logical_shift_left))
                        order.at(m)
                        order.did(v.scalar_tensor_tensor(out=pay[:, :, 2].bitcast(I32), in0=best[1][:].bitcast(I32),
                                                         scalar=0xFFF, in1=whigh[:], op0=ALU.bitwise_and,
                                                         op1=ALU.bitwise_or))
                        order.did(v.scalar_tensor_tensor(out=pay[:, :, 0], in0=blk[:], scalar=float(-GAP),
                                                         in1=jcode[:], op0=ALU.mult, op1=ALU.add))
                        order.did(v.tensor_copy(deg_all[:, bass.ds(t, 1)], deg[:, 0:1]))
                        v.tensor_tensor(pay[:, :, 1], valid[:], rowslot[:], ALU.mult).then_inc(deg_ready, 1)

                    def place(t, s):
                        dve.wait_ge(off_ready, t + 1)
                        dve.wait_ge(adj_counted, t + 1)
                        m = order.did(v.tensor_copy(off[:], ps_off[:, 0:1]))
                        order.at(m)
                        order.did(v.tensor_copy(lane[:], off[:]))
                        order.did(v.tensor_scalar(pos[:], slot_f[:], off[:, 0:1], None, ALU.add))
                        order.did(v.tensor_tensor(end[:], off[:], deg[:, 0:1], ALU.add))
                        order.did(v.scalar_tensor_tensor(out=bad[:], in0=deg[:, 0:1], scalar=nz[s][:, 0:1], in1=bad[:],
                                                         op0=ALU.not_equal, op1=ALU.max))
                        order.at(order.n - 3)
                        order.did(v.tensor_scalar(lane[:], lane[:], 127, None, ALU.bitwise_and))
                        order.at(order.n - 3)
                        order.did(v.tensor_scalar(grp[:], pos[:], 7, None, ALU.logical_shift_right))
                        order.at(order.n - 2)
                        order.did(v.scalar_tensor_tensor(out=bad[:], in0=end[:], scalar=float(E), in1=bad[:],
                                                         op0=ALU.is_gt, op1=ALU.max))
                        order.at(order.n - 1)
                        order.did(v.tensor_tensor(grp_hot[:], grp[:].unsqueeze(2).to_broadcast([R, SLOTS, G]),
                                                  group_i[:].unsqueeze(1).to_broadcast([R, SLOTS, G]), ALU.is_equal))
                        order.did(v.tensor_tensor(lane_hot[:], lane_i[:], lane[:].to_broadcast([R, 128 + SLOTS]),
                                                  ALU.is_equal))
                        order.at(order.n - 1)
                        v.tensor_tensor(rhs_slots, grp_hot[:].unsqueeze(3).to_broadcast([R, SLOTS, G, PAY]),
                                        pay[:].unsqueeze(2).to_broadcast([R, SLOTS, G, PAY]),
                                        ALU.mult).then_inc(slots_ready, 1)

                    def edges(t, s, first):
                        dve.wait_ge(packed, t + 1)
                        if not first:
                            dve.wait_ge(lists_kept, 2 * t - 2)
                            dve.wait_ge(mw_ready, t - 1)
                            dve.wait_ge(hot_turned, t - 1)
                        pk = ps_pack[:, 0:G * PAY].rearrange("p (g a) -> p g a", a=PAY)
                        m = order.did(v.tensor_scalar(node[:], pk[:, :, 0], float(BW), float(BW + N - 1),
                                                      ALU.max, ALU.min))
                        m_rs = order.did(v.tensor_copy(RS[s][:], pk[:, :, 1]))
                        order.at(m)
                        v.tensor_scalar(J[s][:], node[:], float(BW), None, ALU.subtract).then_inc(index_ready, 1)
                        order.at(m_rs)
                        m = order.did(v.tensor_scalar(row_i[:], RS[s][:], 127, None, ALU.bitwise_and))
                        order.did(v.tensor_copy(w_e[s][:], pk[:, :, 2]))
                        order.at(m)
                        m = order.did(v.tensor_copy(row_b[:], row_i[:]))
                        order.at(m)
                        v.tensor_tensor(M[s][:], row_number[:].unsqueeze(1).to_broadcast([128, G, 128]),
                                        row_b[:].unsqueeze(2).to_broadcast([128, G, 128]),
                                        ALU.is_equal).then_inc(hot_ready, 1)

                    def step(t, s, i, now=True, prev=True, first=False):
                        if now:
                            scan_weights(t, s, i)
                        if prev:
                            place(t - 1, 1 - s)
                        if now:
                            scan_columns(t, s)
                        if now:
                            slots(t, s)
                        if prev:
                            edges(t - 1, 1 - s, first)

                    dve.wait_ge(filled, 2)
                    step(0, 0, 0, prev=False)
                    step(1, 1, 0, first=True)
                    a = order.n
                    step(2, 0, 1, first=True)
                    step(3, 1, 1)
                    start = order.n
                    per_pair = start - a
                    with dve.Fori(2, PAIRS) as i:
                        order.base = dve.snap(i * per_pair - 2 * per_pair + start)
                        order.n = 0
                        for s in range(2):
                            step(2 * i + s, s, i)
                        assert order.n == per_pair
                    order.base, order.n = 0, start + (PAIRS - 2) * per_pair
                    step(T, 0, PAIRS, now=False)
                    for n in range(EARLY):
                        dve.wait_ge(gl_ready, TILES_OF[n][1])
                        residual(v, order, gl_all, x_all, norm0, n)

                @block.tensor
                def _(pe):
                    mm, tr = nc.tensor.matmul, nc.tensor.transpose

                    def pack(t):
                        pe.wait_ge(slots_ready, t + 1)
                        for k in range(SLOTS):
                            m = mm(ps_pack, lane_hot[:, SLOTS - k:SLOTS - k + 128],
                                   rhs[:, k * G * PAY:k * G * PAY + WIDE],
                                   start=(k == 0), stop=(k == SLOTS - 1))
                        m.then_inc(packed, 1)

                    def turn(t, s, first):
                        pe.wait_ge(hot_ready, t + 1)
                        if not first:
                            pe.wait_ge(MT_ready, 4 * t)
                        for g in range(G):
                            m = tr(ps_turn[g // 8][:, (g % 8) * 128:(g % 8 + 1) * 128], M[s][:, g, :], ident_bf[:])
                        m.then_inc(hot_turned, 1)

                    def offsets(t):
                        pe.wait_ge(deg_ready, t + 1)
                        mm(ps_off, before[:], deg[:], start=True, stop=True).then_inc(off_ready, 1)

                    def messages(t, s, i, first):
                        pe.wait_ge(MT_ready, 4 * t + 4)
                        pe.wait_ge(gathered[s], 16 * G * (i + 1))
                        for c, (a, b) in enumerate(CHUNKS):
                            if not first:
                                pe.wait_ge(msg_ready, 3 * t + c - 2)
                            for g in range(a, b):
                                o = ps_msg[c][:, (g - a) * D:(g - a + 1) * D]
                                mm(o, MT[s][:, g * 128:(g + 1) * 128], s_all[:, t, :], start=True, stop=False)
                                m = mm(o, ident[:], gath[s][:, g, :], start=False, stop=True)
                            m.then_inc(sums_ready, 1)
                        pe.wait_ge(mw_ready, t + 1)
                        if not first:
                            pe.wait_ge(gl_ready, t)
                        for c, (a, b) in enumerate(CHUNKS):
                            pe.wait_ge(msg_ready, 3 * t + c + 1)
                            for g in range(a, b):
                                m = mm(ps_agg, msg[:, g, :], Mw[s][:, g, 0:R], start=(g == 0), stop=(g == G - 1))
                        m.then_inc(agg_ready, 1)

                    def update(t, first):
                        pe.wait_ge(aggT_ready, t + 1)
                        mm(ps_upd, ident[0:R, 0:R], u_all[:, t, :], start=True, stop=False)
                        mm(ps_upd, aggT[:], updT[:], start=False, stop=True).then_inc(upd_ready, 1)

                    def step(t, s, i, now=True, prev=True, prev2=True, first1=False, first2=False):
                        if prev:
                            pack(t - 1)
                        if now:
                            offsets(t)
                        if prev2:
                            messages(t - 2, s, i - 1, first2)
                            update(t - 2, first2)
                        if prev:
                            turn(t - 1, 1 - s, first1)

                    step(0, 0, 0, prev=False, prev2=False)
                    step(1, 1, 0, prev2=False, first1=True)
                    step(2, 0, 1, first2=True)
                    step(3, 1, 1)
                    with pe.Fori(2, PAIRS) as i:
                        for s in range(2):
                            step(2 * i + s, s, i)
                    step(T, 0, PAIRS, now=False)
                    step(T + 1, 1, PAIRS, now=False, prev=False)

                @block.scalar
                def _(act):
                    a = nc.scalar

                    def gelus(t, s, first):
                        for c, (lo, hi) in enumerate(CHUNKS):
                            act.wait_ge(sums_ready, 3 * t + c + 1)
                            if not first:
                                act.wait_ge(agg_ready, t)
                            a.activation(msg[:, lo:hi, :].rearrange("p g d -> p (g d)"),
                                         ps_msg[c][:, 0:(hi - lo) * D], ACT.Gelu).then_inc(msg_ready, 1)
                        act.wait_ge(agg_ready, t + 1)
                        if not first:
                            act.wait_ge(upd_ready, t)
                        a.copy(aggT[:], ps_agg).then_inc(aggT_ready, 1)
                        act.wait_ge(upd_ready, t + 1)
                        a.activation(gl_all[:, t, :], ps_upd, ACT.Gelu).then_inc(gl_ready, 1)

                    def take_turned(t, s, first):
                        act.wait_ge(hot_turned, t + 1)
                        if not first:
                            act.wait_ge(sums_ready, 3 * t - 3)
                        for n, (lo, hi) in enumerate(((0, 1024), (1024, E))):
                            a.copy(MT[s][:, lo:hi], ps_turn[n][0:R, 0:hi - lo]).then_inc(MT_ready, 1)
                            a.copy(MT_all[:, t, lo:hi], ps_turn[n][0:R, 0:hi - lo]).then_inc(MT_ready, 1)

                    def count(t, s, i, first):
                        act.wait_ge(adj_loaded[s], 16 * i + 16)
                        if not first:
                            act.wait_ge(act_order, 2 * t)
                            act.wait_ge(slots_ready, t - 1)
                        a.activation(sgn[:], adj_t[s][0:R, :], ACT.Sign).then_inc(act_order, 1)
                        act.wait_ge(act_order, 2 * t + 1)
                        a.activation(sgn[:], sgn[:], ACT.Square, accum_out=nz[s][:]).then_inc(adj_counted, 1)
                        act.wait_ge(adj_counted, t + 1)
                        a.sem_inc(act_order, 1)

                    def step(t, s, i, now=True, prev=True, prev2=True, first0=False, first1=False, first2=False):
                        if now:
                            count(t, s, i, first0)
                        if prev2:
                            gelus(t - 2, s, first2)
                        if prev:
                            take_turned(t - 1, 1 - s, first1)

                    step(0, 0, 0, prev=False, prev2=False, first0=True)
                    step(1, 1, 0, prev2=False, first0=True, first1=True)
                    step(2, 0, 1, first1=True, first2=True)
                    step(3, 1, 1)
                    with act.Fori(2, PAIRS) as i:
                        for s in range(2):
                            step(2 * i + s, s, i)
                    step(T, 0, PAIRS, now=False)
                    step(T + 1, 1, PAIRS, now=False, prev=False)
                    act.wait_ge(gl_ready, T)


        with ExitStack() as pf:
            bad_turned = sem("bad_turned", pf)
            flag_ready = sem("flag_ready", pf)
            with nc.Block() as block:
                @block.tensor
                def _(pe):
                    nc.tensor.transpose(ps[0][0:1, 0:R], bad[:], ident[0:R, 0:R]).then_inc(bad_turned, 1)

                @block.vector
                def _(dve):
                    dve.wait_ge(bad_turned, 1)
                    nc.vector.tensor_reduce(flag[:], ps[0][0:1, 0:R], AX.X, ALU.max).then_inc(flag_ready, 1)
                    dve.wait_ge(flag_ready, 1)

        with nc.If(nc.values_load(flag[0:1, 0:1], min_val=0, max_val=1)):
            dense_layer0(nc, sb, sem, ps, adj, adj_t, d_table, s_all, u_all, updT, ident, gl_all, x_all, norm0)
        mid.close()

        qx_all = sb("qx_all", [R, T, 2, D])
        q_parts = sb("q_parts", [R, T, 3, D], BF16)
        zx_all = sb("zx_all", [R, T])
        wg = sb("wg", [R, 2, D])

        with ExitStack() as pm:
            norm1 = Norm(sb, sem, pm, "outer")
            x1 = [sb(f"x1_{s}", [R, D], ctx=pm) for s in range(2)]
            x1T = [sb(f"x1T{s}", [D, R], ctx=pm) for s in range(2)]
            kv_all = sb("kv_all", [R, T, 2 * D], ctx=pm)
            z = [sb(f"zx{s}", [R, 1], ctx=pm) for s in range(2)]
            z_terms = [sb(f"z_terms{s}", [R, D], ctx=pm) for s in range(2)]
            z_bias = sb("z_bias", [R, 1], ctx=pm)
            m_order = sem("m_order", pm)
            normed = sem("normed", pm)
            xb_ready = sem("xb_ready", pm)
            scaled = sem("scaled", pm)
            x1_ready = sem("x1_ready", pm)
            x1_turned = sem("x1_turned", pm)
            x1T_ready = sem("x1T_ready", pm)
            x1_kept = sem("x1_kept", pm)
            proj1 = sem("proj1", pm)
            kv_ready = sem("kv_ready", pm)
            qx_ready = sem("qx_ready", pm)
            z_kept = sem("z_kept", pm)
            z_ready = sem("z_ready", pm)
            kv_stored = sem("kv_stored", pm)
            with nc.Block() as block:
                @block.vector
                def _(dve):
                    v = nc.vector
                    order = Count(dve, m_order)
                    order.did(v.tensor_tensor(wg[:, 0, :], wb[:, 0, :], wb[:, 2, :], ALU.add))
                    m = order.did(v.tensor_tensor(wg[:, 1, :], wb[:, 1, :], wb[:, 2, :], ALU.subtract))
                    order.at(m)
                    order.did(v.tensor_tensor_reduce(out=z_terms[0][:], in0=b1[:, 3, :], in1=wg[:, 1, :], scale=1.0,
                                                     scalar=0.0, op0=ALU.mult, op1=ALU.add, accum_out=z_bias[:]))

                    def add_x(n):
                        a, b = TILES_OF[n]
                        part = gl_all[:, a:b, :]
                        dve.wait_ge(scaled, n + 1)
                        dve.wait_ge(xb_ready, n + 1)
                        m = order.did(v.tensor_tensor(part, part, x_all[:, a:b, :], ALU.add))
                        order.at(m)
                        norm_variances(v, order, gl_all, norm1, n)

                    residual(v, order, gl_all, x_all, norm0, NORM_CHUNKS - 1)
                    for n in range(1, NORM_CHUNKS + 3):
                        if 1 <= n <= NORM_CHUNKS:
                            norm_shifts(v, order, norm0, n - 1)
                        if 2 <= n <= NORM_CHUNKS + 1:
                            add_x(n - 2)
                        if n >= 3:
                            norm_shifts(v, order, norm1, n - 3)
                    order.last()

                    def add_bias(t, s, first):
                        dve.wait_ge(proj1, t + 1)
                        v.tensor_tensor(kv_all[:, t, :], ps[2 + s][0:R, 0:2 * D],
                                        b1[:, 0:2, :].rearrange("p a d -> p (a d)"), ALU.add).then_inc(kv_ready, 1)
                        if not first:
                            dve.wait_ge(z_kept, t - 1)
                        v.tensor_tensor_reduce(out=z_terms[s][:], in0=ps[2 + s][0:R, 3 * D:4 * D], in1=wg[:, 1, :],
                                               scale=1.0, scalar=0.0, op0=ALU.mult, op1=ALU.add,
                                               accum_out=z[s][:]).then_inc(z_ready, 1)
                        v.tensor_tensor(qx_all[:, t, :, :].rearrange("p a d -> p (a d)"), ps[2 + s][0:R, 2 * D:4 * D],
                                        b1[:, 2:4, :].rearrange("p a d -> p (a d)"), ALU.add).then_inc(qx_ready, 1)
                        dve.wait_ge(z_ready, t + 1)
                        v.tensor_tensor(zx_all[:, bass.ds(t, 1)], z[s][:], z_bias[:], ALU.add).then_inc(z_kept, 1)

                    for s in range(2):
                        add_bias(s, s, True)
                    with dve.Fori(1, PAIRS) as i:
                        for s in range(2):
                            add_bias(2 * i + s, s, False)
                    dve.wait_ge(z_kept, T)

                @block.scalar
                def _(act):
                    a_ = nc.scalar
                    for n in range(NORM_CHUNKS + 2):
                        if n < NORM_CHUNKS:
                            norm_deviations(nc.scalar, act, norm0, eps, n)
                        if 1 <= n <= NORM_CHUNKS:
                            norm_rows(nc.scalar, act, gl_all, norm0, n - 1, normed)
                        if n >= 2:
                            norm_deviations(nc.scalar, act, norm1, eps, n - 2)

                    def norm(t, s, first):
                        if not first:
                            act.wait_ge(x1_turned, t - 1)
                            act.wait_ge(x1_kept, t - 1)
                        a_.activation(x1[s][:], gl_all[:, t, :], ACT.Identity, scale=norm1.rstd[:, bass.ds(t, 1)],
                                      bias=norm1.shift[:, bass.ds(t, 1)]).then_inc(x1_ready, 1)

                    def take(t, s, first):
                        act.wait_ge(x1_turned, t + 1)
                        if not first:
                            act.wait_ge(proj1, t - 1)
                        a_.copy(x1T[s][:], ps[s][:, 0:R]).then_inc(x1T_ready, 1)

                    act.wait_ge(norm1.shift_ready, NORM_CHUNKS)
                    norm(0, 0, True)
                    norm(1, 1, True)
                    take(0, 0, True)
                    norm(2, 0, False)
                    take(1, 1, True)
                    with act.Fori(1, PAIRS - 1) as i:
                        norm(2 * i + 1, 1, False)
                        take(2 * i, 0, False)
                        norm(2 * i + 2, 0, False)
                        take(2 * i + 1, 1, False)
                    norm(T - 1, 1, False)
                    take(T - 2, 0, False)
                    take(T - 1, 1, False)

                @block.tensor
                def _(pe):
                    def turn(t, s, first):
                        pe.wait_ge(x1_ready, t + 1)
                        if not first:
                            pe.wait_ge(x1T_ready, t - 1)
                        nc.tensor.transpose(ps[s][:, 0:R], x1[s][:], ident[0:R, 0:R]).then_inc(x1_turned, 1)

                    def project(t, s, first):
                        pe.wait_ge(x1T_ready, t + 1)
                        if not first:
                            pe.wait_ge(qx_ready, t - 1)
                        nc.tensor.matmul(ps[2 + s][0:R, :], x1T[s][:], w1[:].rearrange("p a d -> p (a d)"),
                                         start=True, stop=True).then_inc(proj1, 1)

                    turn(0, 0, True)
                    turn(1, 1, True)
                    project(0, 0, True)
                    turn(2, 0, False)
                    project(1, 1, True)
                    with pe.Fori(1, PAIRS - 1) as i:
                        turn(2 * i + 1, 1, False)
                        project(2 * i, 0, False)
                        turn(2 * i + 2, 0, False)
                        project(2 * i + 1, 1, False)
                    turn(T - 1, 1, False)
                    project(T - 2, 0, False)
                    project(T - 1, 1, False)

                @block.gpsimd
                def _(pool):
                    g = nc.gpsimd
                    def add_ln_b(n):
                        a, b = TILES_OF[n]
                        pool.wait_ge(norm0.h_ready, n + 1)
                        g.tensor_tensor(x_all[:, a:b, :], x_all[:, a:b, :], ln[:, 1:2, :].to_broadcast([R, b - a, D]),
                                        ALU.add).then_inc(xb_ready, 1)

                    def times_ln_w(n):
                        a, b = TILES_OF[n]
                        pool.wait_ge(normed, b)
                        g.tensor_tensor(gl_all[:, a:b, :], gl_all[:, a:b, :],
                                        ln[:, 0:1, :].to_broadcast([R, b - a, D]), ALU.mult).then_inc(scaled, 1)

                    for n in range(NORM_CHUNKS + 1):
                        if n < NORM_CHUNKS:
                            add_ln_b(n)
                        if n >= 1:
                            times_ln_w(n - 1)
                    pool.wait_ge(norm1.var_ready, NORM_CHUNKS)
                    with pool.Fori(0, PAIRS) as i:
                        for s in range(2):
                            pool.wait_ge(x1_ready, 2 * i + s + 1)
                            g.tensor_copy(x_all[:, 2 * i + s, :], x1[s][:]).then_inc(x1_kept, 1)
                    pool.wait_ge(x1_kept, T)

                @block.sync
                def _(sp):
                    kv_rows = kv_table[0:(T - 1) * R, :].rearrange("(t p) d -> p t d", p=R)
                    for a, b, after in STORES:
                        sp.wait_ge(kv_ready, after)
                        sp.dma_start(kv_rows[:, a:b, :], kv_all[:, a:b, :]).then_inc(kv_stored, 16)
                    sp.dma_start(kv_table[(T - 1) * R:N, :], kv_all[0:RL, T - 1, :]).then_inc(kv_stored, 16)
                    sp.wait_ge(kv_stored, 16 * (len(STORES) + 1))

        with ExitStack() as p2:
            J2 = [sb(f"J2_{s}", [128, G], I32, ctx=p2) for s in range(2)]
            MTf = [sb(f"MTf{s}", [R, E], ctx=p2) for s in range(2)]
            KV = [sb(f"KV{s}", [128, G, 2 * D], ctx=p2) for s in range(2)]
            V = [sb(f"V{s}", [128, G, D], ctx=p2) for s in range(2)]
            slot2 = sb("slot2", [128, G], I32, ctx=p2)
            M1 = [sb(f"M1_{s}", [128, G, 128], ctx=p2) for s in range(2)]
            slot_hot = [sb(f"slot_hot{s}", [128, G, SLOTS], ctx=p2) for s in range(2)]
            prod = sb("prod", [128, G, D], ctx=p2)
            sc = [sb(f"sc{s}", [128, G, H], ctx=p2) for s in range(2)]
            by_slot = sb("by_slot", [128, G * SLOTS * H + WIDE], ctx=p2)
            by_slot_edges = by_slot[:, 0:G * SLOTS * H].rearrange("p (g k h) -> p g k h", g=G, k=SLOTS)
            past = sb("past", [R, SLOTS], ctx=p2)
            masked = sb("masked", [R, SLOTS, H], ctx=p2)
            top = sb("top", [R, WIDE], ctx=p2)
            below = sb("below", [128, G, H], ctx=p2)
            PV = sb("PV", [128, G, D + H], ctx=p2)
            gate = Gate(sb, p2, "lists")

            rows_ready = sem("rows_ready", p2)
            v_kept = sem("v_kept", p2)
            MTf_ready = sem("MTf_ready", p2)
            q_rounded = sem("q_rounded", p2)
            q_reduced = sem("q_reduced", p2)
            turned_back = sem("turned_back", p2)
            M1_ready = sem("M1_ready", p2)
            kv_in = [sem(f"kv_in{s}", p2) for s in range(2)]
            q_spread = sem("q_spread", p2)
            prod_done = sem("prod_done", p2)
            by_slot_ready = sem("by_slot_ready", p2)
            slotted = sem("slotted", p2)
            top_ready = sem("top_ready", p2)
            top_spread = sem("top_spread", p2)
            below_ready = sem("below_ready", p2)
            p_ready = sem("p_ready", p2)
            pv_ready = sem("pv_ready", p2)
            att_ready = sem("att_ready", p2)
            att_read = sem("att_read", p2)
            z_ready = sem("z_ready", p2)
            ez_ready = sem("ez_ready", p2)
            order2 = sem("order2", p2)
            pe_passed = sem("pe_passed", p2)
            passed2 = sem("passed2", p2)

            ps_q, ps_slot, ps_top = ps[0:3], ps[3][0:R, 0:WIDE], ps[4][:, 0:(G - 1) * H + WIDE]
            ps_att = ps[5][0:R, 0:D + H]
            ps_hot = [ps[n][:].bitcast(BF16) for n in (6, 7)]
            Q_HALVES = ((0, T // 2), (T // 2, T))

            with nc.Block() as block:
                @block.gpsimd
                def _(pool):
                    def gather(t, s, first):
                        pool.wait_ge(rows_ready, t + 1)
                        if not first:
                            pool.wait_ge(prod_done, 3 * t - 3)
                            pool.wait_ge(v_kept, t - 1)
                        pool.sem_inc(passed2)
                        for g in range(G):
                            pool.indirect_dma_start(
                                out=KV[s][:, g, :], out_offset=None, in_=kv_table,
                                in_offset=bass.IndirectOffsetOnAxis(ap=J2[s][:, g:g + 1], axis=0),
                            ).then_inc(kv_in[s], 16)

                    for s in range(2):
                        gather(s, s, True)
                    with pool.Fori(1, PAIRS) as i:
                        for s in range(2):
                            gather(2 * i + s, s, False)

                @block.scalar
                def _(act):
                    a = nc.scalar

                    def rows(t, s, i, first):
                        if not first:
                            act.wait_ge(kv_in[s], 16 * G * i)
                        a.copy(J2[s][:], J_all[:, t, :]).then_inc(rows_ready, 1)

                    def hot_rows(t, s, first):
                        if not first:
                            act.wait_ge(top_spread, t - 1)
                        a.copy(MTf[s][:], MT_all[:, t, :]).then_inc(MTf_ready, 1)

                    def hot_edges(t, s):
                        act.wait_ge(turned_back, t + 1)
                        for n, (lo, hi) in enumerate(((0, 8), (8, G))):
                            a.copy(M1[s][:, lo:hi, 0:R], ps_hot[n][:, 0:(hi - lo) * 128].rearrange(
                                "p (g r) -> p g r", r=128)[:, :, 0:R]).then_inc(M1_ready, 1)

                    def keep_v(t, s, i, first):
                        act.wait_ge(kv_in[s], 16 * G * i + 16 * G)
                        if not first:
                            act.wait_ge(pv_ready, t - 1)
                        a.copy(V[s][:], KV[s][:, :, D:2 * D]).then_inc(v_kept, 1)

                    def exps(t, first):
                        act.wait_ge(below_ready, t + 1)
                        if not first:
                            act.wait_ge(att_ready, t)
                        a.activation(PV[:, :, D:D + H], below[:], ACT.Exp, scale=SCALE).then_inc(p_ready, 1)

                    def gates(t):
                        act.wait_ge(z_ready, t + 1)
                        a.activation(gate.ez[:], gate.z2[:], ACT.Exp, scale=-1.0).then_inc(ez_ready, 1)

                    def step(t, s, i, prev=True, more3=True, more2=True, more1=True, first=False):
                        if more1:
                            if not first:
                                hot_edges(t + 1, 1 - s)
                        if more1:
                            keep_v(t + 1, 1 - s, i + s, first)
                        if more3:
                            rows(t + 3, 1 - s, i + 1 + s, False)
                        if more2:
                            hot_rows(t + 2, s, False)
                        if prev:
                            gates(t - 1)
                        exps(t, first)

                    for s in range(2):
                        rows(s, s, 0, True)
                    for n in range(2):
                        for k, (lo, hi) in enumerate(Q_HALVES):
                            if n > 0:
                                act.wait_ge(q_reduced, k + 1)
                            a.copy(q_parts[:, lo:hi, n, :], qx_all[:, lo:hi, 0, :]).then_inc(q_rounded, 1)
                    for s in range(2):
                        hot_edges(s, s)
                        hot_rows(s, s, True)
                    keep_v(0, 0, 0, True)
                    rows(2, 0, 1, False)
                    step(0, 0, 0, prev=False, first=True)
                    step(1, 1, 0)
                    with act.Fori(1, PAIRS - 2) as i:
                        for s in range(2):
                            step(2 * i + s, s, i)
                    step(T - 4, 0, PAIRS - 2)
                    step(T - 3, 1, PAIRS - 2, more3=False)
                    step(T - 2, 0, PAIRS - 1, more3=False, more2=False)
                    step(T - 1, 1, PAIRS - 1, more3=False, more2=False, more1=False)
                    gates(T - 1)

                @block.tensor
                def _(pe):
                    mm = nc.tensor.matmul

                    def spread_q(t, s, first):
                        for c, (a, b) in enumerate(CHUNKS):
                            if not first:
                                pe.wait_ge(prod_done, 3 * t - 2 + c)
                            for g in range(a, b):
                                for n in range(3):
                                    m = mm(ps_q[c][:, (g - a) * D:(g - a + 1) * D],
                                           MT_all[:, t, g * 128:(g + 1) * 128], q_parts[:, t, n, :],
                                           start=(n == 0), stop=(n == 2))
                            m.then_inc(q_spread, 1)

                    def turn_back(t, first):
                        if not first:
                            pe.wait_ge(M1_ready, 2 * t)
                            pe.sem_inc(pe_passed)
                        for g in range(G):
                            m = nc.tensor.transpose(ps_hot[g // 8][:, (g % 8) * 128:(g % 8) * 128 + R],
                                                    MT_all[:, t, g * 128:(g + 1) * 128], ident_bf[0:R, 0:R])
                        m.then_inc(turned_back, 1)

                    def spread_slot(t, s):
                        pe.wait_ge(M1_ready, 2 * t + 2)
                        pe.wait_ge(by_slot_ready, t + 1)
                        for g in range(G):
                            m = mm(ps_slot, M1[s][:, g, 0:R], by_slot[:, g * SLOTS * H:g * SLOTS * H + WIDE],
                                   start=(g == 0), stop=(g == G - 1))
                        m.then_inc(slotted, 1)

                    def spread_top(t, s):
                        pe.wait_ge(MTf_ready, t + 1)
                        pe.wait_ge(top_ready, t + 1)
                        for g in range(G):
                            m = mm(ps_top[:, g * H:g * H + WIDE], MTf[s][:, g * 128:(g + 1) * 128], top[:],
                                   start=True, stop=True)
                        m.then_inc(top_spread, 1)

                    def attend(t, s, first):
                        pe.wait_ge(pv_ready, t + 1)
                        if not first:
                            pe.wait_ge(att_read, t)
                        for g in range(G):
                            m = mm(ps_att, M1[s][:, g, 0:R], PV[:, g, :], start=(g == 0), stop=(g == G - 1))
                        m.then_inc(att_ready, 1)

                    def step(t, s, first=False, more2=True, more1=True):
                        spread_top(t, s)
                        if more2:
                            spread_q(t + 2, s, False)
                        if more1:
                            spread_slot(t + 1, 1 - s)
                        attend(t, s, first)
                        if more2:
                            turn_back(t + 2, False)

                    turn_back(0, True)
                    turn_back(1, False)
                    pe.wait_ge(q_reduced, 3)
                    spread_q(0, 0, True)
                    pe.wait_ge(q_reduced, 4)
                    spread_slot(0, 0)
                    spread_q(1, 1, False)
                    step(0, 0, first=True)
                    step(1, 1)
                    with pe.Fori(1, PAIRS - 1) as i:
                        for s in range(2):
                            step(2 * i + s, s)
                    step(T - 2, 0, more2=False)
                    step(T - 1, 1, more2=False, more1=False)

                @block.vector
                def _(dve):
                    v = nc.vector
                    order = Count(dve, order2)

                    def scores(t, s, i):
                        for c, (a, b) in enumerate(CHUNKS):
                            dve.wait_ge(q_spread, 3 * t + c + 1)
                            if c == 0:
                                dve.wait_ge(kv_in[s], 16 * G * i + 16 * G)
                            v.tensor_tensor(prod[:, a:b, :], KV[s][:, a:b, 0:D],
                                            ps_q[c][:, 0:(b - a) * D].rearrange("p (g d) -> p g d", d=D),
                                            ALU.mult).then_inc(prod_done, 1)
                        dve.wait_ge(prod_done, 3 * t + 3)
                        return order.did(v.tensor_reduce(sc[s][:].rearrange("p g h -> p (g h)"),
                                                         prod[:].rearrange("p g (h c) -> p (g h) c", c=HC),
                                                         AX.X, ALU.add))

                    def spread_slots(t, s, scored):
                        order.at(scored)
                        v.tensor_tensor(by_slot_edges, slot_hot[s][:].unsqueeze(3).to_broadcast([128, G, SLOTS, H]),
                                        sc[s][:].unsqueeze(2).to_broadcast([128, G, SLOTS, H]),
                                        ALU.mult).then_inc(by_slot_ready, 1)

                    def slots_of(t, s):
                        m = order.did(v.tensor_scalar(slot2[:], RS_all[:, t, :], 7, None, ALU.logical_shift_right))
                        order.at(m)
                        order.did(v.tensor_tensor(slot_hot[s][:], slot_of[:].unsqueeze(1).to_broadcast([128, G, SLOTS]),
                                                  slot2[:].unsqueeze(2).to_broadcast([128, G, SLOTS]), ALU.is_equal))

                    def maximum(t, s):
                        m = order.did(v.tensor_tensor(past[:], slot_f[:], deg_all[:, bass.ds(t, 1)].to_broadcast([R, SLOTS]),
                                                      ALU.is_ge))
                        order.at(m)
                        dve.wait_ge(slotted, t + 1)
                        m = order.did(v.scalar_tensor_tensor(out=masked[:], in0=past[:].unsqueeze(2).to_broadcast([R, SLOTS, H]),
                                                             scalar=NEG, in1=ps_slot[:, 0:SLOTS * H].rearrange("p (k h) -> p k h", h=H),
                                                             op0=ALU.mult, op1=ALU.add))
                        order.at(m)
                        v.tensor_reduce(top[:, 0:H], masked[:].rearrange("p k h -> p h k"), AX.X, ALU.max).then_inc(top_ready, 1)

                    def subtract(t, s):
                        dve.wait_ge(top_spread, t + 1)
                        v.tensor_tensor(below[:].rearrange("p g h -> p (g h)"), sc[s][:].rearrange("p g h -> p (g h)"),
                                        ps_top[:, 0:G * H], ALU.subtract).then_inc(below_ready, 1)

                    def weigh(t, s):
                        dve.wait_ge(p_ready, t + 1)
                        v.tensor_tensor(PV[:, :, 0:D].rearrange("p g (h c) -> p g h c", c=HC),
                                        V[s][:].rearrange("p g (h c) -> p g h c", c=HC),
                                        PV[:, :, D:D + H].unsqueeze(3).to_broadcast([128, G, H, HC]),
                                        ALU.mult).then_inc(pv_ready, 1)

                    def step(t, s, i, now=True, more=True, prev=True, prev2=True):
                        if more:
                            slots_of(t + 1, 1 - s)
                        if now:
                            maximum(t, s)
                        if prev2:
                            dve.wait_ge(ez_ready, t - 1)
                            mix(v, order, x_all[:, t - 2, :], gl_all[:, t - 2, :], gate)
                        if prev:
                            dve.wait_ge(att_ready, t)
                            outcome(v, order, ps_att[:, 0:D], ps_att[:, D:D + H], att_read, t, wg,
                                    zx_all[:, bass.ds(t - 1, 1)], qx_all[:, t - 1, 1, :], gate, z_ready)
                        if more:
                            scored = scores(t + 1, 1 - s, i + s)
                        if now:
                            subtract(t, s)
                        if more:
                            spread_slots(t + 1, 1 - s, scored)
                        if now:
                            weigh(t, s)

                    order.did(v.memset(top[:], 0.0))
                    order.did(v.memset(by_slot[:, G * SLOTS * H:], 0.0))
                    slots_of(0, 0)
                    for n in range(2):
                        for k, (lo, hi) in enumerate(Q_HALVES):
                            dve.wait_ge(q_rounded, 2 * n + k + 1)
                            left = qx_all[:, lo:hi, 0, :] if n == 0 else q_parts[:, lo:hi, 2, :]
                            v.tensor_tensor(left, qx_all[:, lo:hi, 0, :], q_parts[:, lo:hi, n, :],
                                            ALU.subtract).then_inc(q_reduced, 1)
                    scored = scores(0, 0, 0)
                    order.last()
                    spread_slots(0, 0, scored)
                    step(0, 0, 0, prev=False, prev2=False)
                    step(1, 1, 0, prev2=False)
                    start = order.n
                    with dve.Fori(1, PAIRS - 1) as i:
                        per_pair = 26
                        order.base = dve.snap(i * per_pair + (start - per_pair))
                        order.n = 0
                        for s in range(2):
                            step(2 * i + s, s, i)
                        assert order.n == per_pair, order.n
                    order.base, order.n = 0, start + (PAIRS - 2) * per_pair
                    step(T - 2, 0, PAIRS - 1)
                    step(T - 1, 1, PAIRS - 1, more=False)
                    step(T, 0, PAIRS, now=False, more=False)
                    step(T + 1, 1, PAIRS, now=False, more=False, prev=False)
                    order.last()

        with nc.If(nc.values_load(flag[0:1, 0:1], min_val=0, max_val=1)):
            dense_layer1(nc, sb, sem, ps, adj, kv_table, qx_all, q_parts, zx_all, wg, x_all, ident, gl_all)

        with ExitStack() as p3:
            norm2 = Norm(sb, sem, p3, "last")
            order3 = sem("order3", p3)
            out_ready = sem("out_ready", p3)
            late_ready = sem("late_ready", p3)
            stored = sem("stored", p3)
            with nc.Block() as block:
                @block.vector
                def _(dve):
                    v = nc.vector
                    order = Count(dve, order3)
                    for n in range(NORM_CHUNKS + 1):
                        if n < NORM_CHUNKS:
                            norm_variances(v, order, gl_all, norm2, n)
                        if n >= 1:
                            norm_shifts(v, order, norm2, n - 1)
                    for n in range(NORM_CHUNKS // 2, NORM_CHUNKS):
                        dve.wait_ge(norm2.shift_ready, n + 1)
                        for t in range(*TILES_OF[n]):
                            v.tensor_scalar(gl_all[:, t, :], gl_all[:, t, :], norm2.rstd[:, t:t + 1],
                                            norm2.shift[:, t:t + 1], ALU.mult, ALU.add).then_inc(late_ready, 1)

                @block.scalar
                def _(act):
                    for n in range(NORM_CHUNKS):
                        norm_deviations(nc.scalar, act, norm2, eps, n)
                        if 1 <= n <= NORM_CHUNKS // 2:
                            norm_rows(nc.scalar, act, gl_all, norm2, n - 1, out_ready)

                @block.sync
                def _(sp):
                    rows = out[0:(T - 1) * R, :].rearrange("(t p) d -> p t d", p=R)
                    half = TILES_OF[NORM_CHUNKS // 2][0]
                    for a, b in TILES_OF:
                        if b <= half:
                            sp.wait_ge(out_ready, b)
                        else:
                            sp.wait_ge(late_ready, b - half)
                        b = min(b, T - 1)
                        sp.dma_start(rows[:, a:b, :], gl_all[:, a:b, :]).then_inc(stored, 16)
                    sp.dma_start(out[(T - 1) * R:N, :], gl_all[0:RL, T - 1, :]).then_inc(stored, 16)
                    sp.wait_ge(stored, 16 * (NORM_CHUNKS + 1))


_INS = ['x', 'adj', 'L0_gnn_msg_w', 'L0_gnn_msg_b', 'L0_gnn_upd_w', 'L0_gnn_upd_b', 'L0_gnn_ln_w', 'L0_gnn_ln_b',
        'L1_gnn_Wq', 'L1_gnn_bq', 'L1_gnn_Wk', 'L1_gnn_bk', 'L1_gnn_Wv', 'L1_gnn_bv', 'L1_gnn_Ws', 'L1_gnn_bs',
        'L1_gnn_Wb']


def kernel(**inputs):
    import numpy as _np
    import concourse.bacc as _bacc
    from concourse import mybir as _mybir
    from concourse.bass_utils import run_bass_kernel_spmd as _run

    nc = _bacc.Bacc("TRN2", target_bir_lowering=False, num_devices=1)
    arrays, args = {}, []
    for name in _INS:
        a = _np.ascontiguousarray(inputs[name])
        arrays[f"in_{name}_dram"] = a
        args.append(nc.dram_tensor(f"in_{name}_dram", a.shape, _mybir.dt.from_np(a.dtype), kind="ExternalInput").ap())
    args.append(nc.dram_tensor("out_0_dram", (N, D), _mybir.dt.from_np(_np.dtype("float32")),
                               kind="ExternalOutput").ap())
    adj_resnorm_kernel(nc, *args)
    r = _run(nc, [arrays], core_ids=[0])
    return r.results[0]["out_0_dram"]
```
